# Optimizing a Trainium2 kernel written in Bass

```python
import numpy as np
import jax
import jax.numpy as jnp

def _softmax(x, axis=-1):
    return jax.nn.softmax(x, axis=axis)

def _gelu(x):
    return jax.nn.gelu(x, approximate=True)

def _silu(x):
    return jax.nn.silu(x)

def _sigmoid(x):
    return jax.nn.sigmoid(x)

def _layernorm(x, axis=-1, eps=1e-05):
    m = jnp.mean(x, axis=axis, keepdims=True)
    v = jnp.var(x, axis=axis, keepdims=True)
    return (x - m) / jnp.sqrt(v + eps)

def _scatter_add(tgt, idx, src, axis=0):
    return tgt.at[idx].add(src)

def _segment_sum(src, seg, n):
    return jax.ops.segment_sum(src, seg, n)
kernel_name = 'mk_xattn_seq_d2_seqx_r4_7a4cc7'

def setup_inputs(seed: int=0):
    np.random.seed(seed)
    _w = jnp.asarray

    def _rec_inputs():
        import jax
        import jax.numpy as jnp
        _rk = jax.random.key(seed)
        x = 7.22e-05 + 1 * jax.random.normal(jax.random.fold_in(_rk, 1), (2, 1024, 256), jnp.float32)
        _lenS = 1024 - jax.random.randint(jax.random.fold_in(_rk, 7), (2,), 0, max(1, 1024 // 4) + 1, jnp.int32)
        _lenS2 = 77 - jax.random.randint(jax.random.fold_in(_rk, 8), (2,), 0, max(1, 77 // 4) + 1, jnp.int32)
        _ctx_768P = jax.random.normal(jax.random.fold_in(_rk, 11), (2, 16, 192), jnp.float32)
        _ctx_768c = jax.random.dirichlet(jax.random.fold_in(_rk, 511), 0.3 * jnp.ones((16,), jnp.float32), (2, 77))
        _ctx_768t = jnp.einsum('bsk,bkd->bsd', _ctx_768c, _ctx_768P)
        _ctx_768t = _ctx_768t * jax.lax.rsqrt(jnp.mean(jnp.square(_ctx_768t)) + 1e-12) * 0.953939
        ctx_768 = 0.00272024 + 0.999456 * (_ctx_768t + 0.3 * jax.random.normal(jax.random.fold_in(_rk, 611), (2, 77, 192), jnp.float32))
        return (x, ctx_768)
    x, ctx_768 = _rec_inputs()

    def _L0_xattn_setup():
        import jax, jax.numpy as jnp
        import numpy as np
        DIM = 256
        HEADS = 16
        D_HEAD = 64
        CTX_DIM = 192
        FF_INNER = 4 * DIM

        def layer_norm(x, g, b, eps=1e-05):
            m = jnp.mean(x, axis=-1, keepdims=True)
            v = jnp.var(x, axis=-1, keepdims=True)
            return (x - m) * jax.lax.rsqrt(v + eps) * g + b

        def attention(x, ctx, wq, wk, wv, wo, bo):
            q = x @ wq
            k = ctx @ wk
            v = ctx @ wv
            b, n, _ = q.shape
            m = k.shape[1]
            q = q.reshape(b, n, HEADS, D_HEAD).transpose(0, 2, 1, 3)
            k = k.reshape(b, m, HEADS, D_HEAD).transpose(0, 2, 1, 3)
            v = v.reshape(b, m, HEADS, D_HEAD).transpose(0, 2, 1, 3)
            scale = D_HEAD ** (-0.5)
            sim = jnp.einsum('bhid,bhjd->bhij', q.astype(jnp.float32), k.astype(jnp.float32)) * scale
            attn = jax.nn.softmax(sim, axis=-1).astype(v.dtype)
            out = jnp.einsum('bhij,bhjd->bhid', attn, v)
            out = out.transpose(0, 2, 1, 3).reshape(b, n, HEADS * D_HEAD)
            return out @ wo + bo

        def geglu_ff(x, w1, b1, w2, b2):
            h = x @ w1 + b1
            a, gate = jnp.split(h, 2, axis=-1)
            return a * jax.nn.gelu(gate, approximate=False) @ w2 + b2
        key = jax.random.key(seed)
        ks = jax.random.split(key, 16)
        s = 0.02
        inp = {'x': jax.random.normal(ks[0], (8, 256, DIM), jnp.float32), 'context': jax.random.normal(ks[1], (8, 77, CTX_DIM), jnp.float32), 'wq1': jax.random.normal(ks[2], (DIM, HEADS * D_HEAD), jnp.float32) * s, 'wk1': jax.random.normal(ks[3], (DIM, HEADS * D_HEAD), jnp.float32) * s, 'wv1': jax.random.normal(ks[4], (DIM, HEADS * D_HEAD), jnp.float32) * s, 'wo1': jax.random.normal(ks[5], (HEADS * D_HEAD, DIM), jnp.float32) * s, 'bo1': jnp.zeros((DIM,), jnp.float32), 'wq2': jax.random.normal(ks[6], (DIM, HEADS * D_HEAD), jnp.float32) * s, 'wk2': jax.random.normal(ks[7], (CTX_DIM, HEADS * D_HEAD), jnp.float32) * s, 'wv2': jax.random.normal(ks[8], (CTX_DIM, HEADS * D_HEAD), jnp.float32) * s, 'wo2': jax.random.normal(ks[9], (HEADS * D_HEAD, DIM), jnp.float32) * s, 'bo2': jnp.zeros((DIM,), jnp.float32), 'w_ff1': jax.random.normal(ks[10], (DIM, 2 * FF_INNER), jnp.float32) * s, 'b_ff1': jnp.zeros((2 * FF_INNER,), jnp.float32), 'w_ff2': jax.random.normal(ks[11], (FF_INNER, DIM), jnp.float32) * s, 'b_ff2': jnp.zeros((DIM,), jnp.float32), 'g1': jnp.ones((DIM,), jnp.float32), 'b1': jnp.zeros((DIM,), jnp.float32), 'g2': jnp.ones((DIM,), jnp.float32), 'b2': jnp.zeros((DIM,), jnp.float32), 'g3': jnp.ones((DIM,), jnp.float32), 'b3': jnp.zeros((DIM,), jnp.float32)}
        return inp
    _L0_xattn_all = _L0_xattn_setup()
    _L0_xattn_in = {k: v for k, v in _L0_xattn_all.items() if k in ('wq1', 'wk1', 'wv1', 'wo1', 'bo1', 'wq2', 'wk2', 'wv2', 'wo2', 'bo2', 'w_ff1', 'b_ff1', 'w_ff2', 'b_ff2', 'g1', 'b1', 'g2', 'b2', 'g3', 'b3')}
    del _L0_xattn_all

    def _L1_xattn_setup():
        import jax, jax.numpy as jnp
        import numpy as np
        D_MODEL = 256
        D_COND = 192
        N_HEADS = 16
        D_HEAD = 64
        D_ATTN = N_HEADS * D_HEAD
        D_FF = 4 * D_MODEL

        def _layernorm(x, g, b, eps=1e-05):
            mu = jnp.mean(x, axis=-1, keepdims=True)
            var = jnp.var(x, axis=-1, keepdims=True)
            return (x - mu) * jax.lax.rsqrt(var + eps) * g + b

        def _attention(xq, xkv, wq, wk, wv, wo, bo):
            B, S, _ = xq.shape
            T = xkv.shape[1]
            q = (xq @ wq).reshape(B, S, N_HEADS, D_HEAD)
            k = (xkv @ wk).reshape(B, T, N_HEADS, D_HEAD)
            v = (xkv @ wv).reshape(B, T, N_HEADS, D_HEAD)
            scale = D_HEAD ** (-0.5)
            attn = jnp.einsum('bihd,bjhd->bhij', q, k) * scale
            attn = jax.nn.softmax(attn, axis=-1)
            out = jnp.einsum('bhij,bjhd->bihd', attn, v).reshape(B, S, D_ATTN)
            return out @ wo + bo
        key = jax.random.key(seed)
        ks = jax.random.split(key, 16)
        B, S, T = (8, 256, 64)
        n = jax.random.normal
        inp = {'x': n(ks[0], (B, S, D_MODEL), jnp.float32), 'cond_emb': n(ks[1], (B, T, D_COND), jnp.float32), 'ln1_g': jnp.ones((D_MODEL,), jnp.float32), 'ln1_b': jnp.zeros((D_MODEL,), jnp.float32), 'ln2_g': jnp.ones((D_MODEL,), jnp.float32), 'ln2_b': jnp.zeros((D_MODEL,), jnp.float32), 'ln3_g': jnp.ones((D_MODEL,), jnp.float32), 'ln3_b': jnp.zeros((D_MODEL,), jnp.float32), 'sa_wq': n(ks[2], (D_MODEL, D_ATTN), jnp.float32) * D_MODEL ** (-0.5), 'sa_wk': n(ks[3], (D_MODEL, D_ATTN), jnp.float32) * D_MODEL ** (-0.5), 'sa_wv': n(ks[4], (D_MODEL, D_ATTN), jnp.float32) * D_MODEL ** (-0.5), 'sa_wo': n(ks[5], (D_ATTN, D_MODEL), jnp.float32) * D_ATTN ** (-0.5), 'sa_bo': jnp.zeros((D_MODEL,), jnp.float32), 'ca_wq': n(ks[6], (D_MODEL, D_ATTN), jnp.float32) * D_MODEL ** (-0.5), 'ca_wk': n(ks[7], (D_COND, D_ATTN), jnp.float32) * D_COND ** (-0.5), 'ca_wv': n(ks[8], (D_COND, D_ATTN), jnp.float32) * D_COND ** (-0.5), 'ca_wo': n(ks[9], (D_ATTN, D_MODEL), jnp.float32) * D_ATTN ** (-0.5), 'ca_bo': jnp.zeros((D_MODEL,), jnp.float32), 'ff_w1': n(ks[10], (D_MODEL, 2 * D_FF), jnp.float32) * D_MODEL ** (-0.5), 'ff_b1': jnp.zeros((2 * D_FF,), jnp.float32), 'ff_w2': n(ks[11], (D_FF, D_MODEL), jnp.float32) * D_FF ** (-0.5), 'ff_b2': jnp.zeros((D_MODEL,), jnp.float32)}
        return inp
    _L1_xattn_all = _L1_xattn_setup()
    _L1_xattn_in = {k: v for k, v in _L1_xattn_all.items() if k in ('ln1_g', 'ln1_b', 'ln2_g', 'ln2_b', 'ln3_g', 'ln3_b', 'sa_wq', 'sa_wk', 'sa_wv', 'sa_wo', 'sa_bo', 'ca_wq', 'ca_wk', 'ca_wv', 'ca_wo', 'ca_bo', 'ff_w1', 'ff_b1', 'ff_w2', 'ff_b2')}
    del _L1_xattn_all
    return {'x': x, 'ctx_768': ctx_768, 'L0_xattn_wq1': _L0_xattn_in['wq1'], 'L0_xattn_wk1': _L0_xattn_in['wk1'], 'L0_xattn_wv1': _L0_xattn_in['wv1'], 'L0_xattn_wo1': _L0_xattn_in['wo1'], 'L0_xattn_bo1': _L0_xattn_in['bo1'], 'L0_xattn_wq2': _L0_xattn_in['wq2'], 'L0_xattn_wk2': _L0_xattn_in['wk2'], 'L0_xattn_wv2': _L0_xattn_in['wv2'], 'L0_xattn_wo2': _L0_xattn_in['wo2'], 'L0_xattn_bo2': _L0_xattn_in['bo2'], 'L0_xattn_w_ff1': _L0_xattn_in['w_ff1'], 'L0_xattn_b_ff1': _L0_xattn_in['b_ff1'], 'L0_xattn_w_ff2': _L0_xattn_in['w_ff2'], 'L0_xattn_b_ff2': _L0_xattn_in['b_ff2'], 'L0_xattn_g1': _L0_xattn_in['g1'], 'L0_xattn_b1': _L0_xattn_in['b1'], 'L0_xattn_g2': _L0_xattn_in['g2'], 'L0_xattn_b2': _L0_xattn_in['b2'], 'L0_xattn_g3': _L0_xattn_in['g3'], 'L0_xattn_b3': _L0_xattn_in['b3'], 'L1_xattn_ln1_g': _L1_xattn_in['ln1_g'], 'L1_xattn_ln1_b': _L1_xattn_in['ln1_b'], 'L1_xattn_ln2_g': _L1_xattn_in['ln2_g'], 'L1_xattn_ln2_b': _L1_xattn_in['ln2_b'], 'L1_xattn_ln3_g': _L1_xattn_in['ln3_g'], 'L1_xattn_ln3_b': _L1_xattn_in['ln3_b'], 'L1_xattn_sa_wq': _L1_xattn_in['sa_wq'], 'L1_xattn_sa_wk': _L1_xattn_in['sa_wk'], 'L1_xattn_sa_wv': _L1_xattn_in['sa_wv'], 'L1_xattn_sa_wo': _L1_xattn_in['sa_wo'], 'L1_xattn_sa_bo': _L1_xattn_in['sa_bo'], 'L1_xattn_ca_wq': _L1_xattn_in['ca_wq'], 'L1_xattn_ca_wk': _L1_xattn_in['ca_wk'], 'L1_xattn_ca_wv': _L1_xattn_in['ca_wv'], 'L1_xattn_ca_wo': _L1_xattn_in['ca_wo'], 'L1_xattn_ca_bo': _L1_xattn_in['ca_bo'], 'L1_xattn_ff_w1': _L1_xattn_in['ff_w1'], 'L1_xattn_ff_b1': _L1_xattn_in['ff_b1'], 'L1_xattn_ff_w2': _L1_xattn_in['ff_w2'], 'L1_xattn_ff_b2': _L1_xattn_in['ff_b2']}

def reference(x, ctx_768, L0_xattn_wq1, L0_xattn_wk1, L0_xattn_wv1, L0_xattn_wo1, L0_xattn_bo1, L0_xattn_wq2, L0_xattn_wk2, L0_xattn_wv2, L0_xattn_wo2, L0_xattn_bo2, L0_xattn_w_ff1, L0_xattn_b_ff1, L0_xattn_w_ff2, L0_xattn_b_ff2, L0_xattn_g1, L0_xattn_b1, L0_xattn_g2, L0_xattn_b2, L0_xattn_g3, L0_xattn_b3, L1_xattn_ln1_g, L1_xattn_ln1_b, L1_xattn_ln2_g, L1_xattn_ln2_b, L1_xattn_ln3_g, L1_xattn_ln3_b, L1_xattn_sa_wq, L1_xattn_sa_wk, L1_xattn_sa_wv, L1_xattn_sa_wo, L1_xattn_sa_bo, L1_xattn_ca_wq, L1_xattn_ca_wk, L1_xattn_ca_wv, L1_xattn_ca_wo, L1_xattn_ca_bo, L1_xattn_ff_w1, L1_xattn_ff_b1, L1_xattn_ff_w2, L1_xattn_ff_b2):
    import jax
    import jax.numpy as jnp

    def _L0_xattn_ref(x, context, wq1, wk1, wv1, wo1, bo1, wq2, wk2, wv2, wo2, bo2, w_ff1, b_ff1, w_ff2, b_ff2, g1, b1, g2, b2, g3, b3):
        import jax, jax.numpy as jnp
        import numpy as np
        DIM = 256
        HEADS = 16
        D_HEAD = 64
        CTX_DIM = 192
        FF_INNER = 4 * DIM

        def layer_norm(x, g, b, eps=1e-05):
            m = jnp.mean(x, axis=-1, keepdims=True)
            v = jnp.var(x, axis=-1, keepdims=True)
            return (x - m) * jax.lax.rsqrt(v + eps) * g + b

        def attention(x, ctx, wq, wk, wv, wo, bo):
            q = x @ wq
            k = ctx @ wk
            v = ctx @ wv
            b, n, _ = q.shape
            m = k.shape[1]
            q = q.reshape(b, n, HEADS, D_HEAD).transpose(0, 2, 1, 3)
            k = k.reshape(b, m, HEADS, D_HEAD).transpose(0, 2, 1, 3)
            v = v.reshape(b, m, HEADS, D_HEAD).transpose(0, 2, 1, 3)
            scale = D_HEAD ** (-0.5)
            sim = jnp.einsum('bhid,bhjd->bhij', q.astype(jnp.float32), k.astype(jnp.float32)) * scale
            attn = jax.nn.softmax(sim, axis=-1).astype(v.dtype)
            out = jnp.einsum('bhij,bhjd->bhid', attn, v)
            out = out.transpose(0, 2, 1, 3).reshape(b, n, HEADS * D_HEAD)
            return out @ wo + bo

        def geglu_ff(x, w1, b1, w2, b2):
            h = x @ w1 + b1
            a, gate = jnp.split(h, 2, axis=-1)
            return a * jax.nn.gelu(gate, approximate=False) @ w2 + b2
        x = x + attention(layer_norm(x, g1, b1), layer_norm(x, g1, b1), wq1, wk1, wv1, wo1, bo1)
        x = x + attention(layer_norm(x, g2, b2), context, wq2, wk2, wv2, wo2, bo2)
        x = x + geglu_ff(layer_norm(x, g3, b3), w_ff1, b_ff1, w_ff2, b_ff2)
        return x

    def _L1_xattn_ref(x, cond_emb, ln1_g, ln1_b, ln2_g, ln2_b, ln3_g, ln3_b, sa_wq, sa_wk, sa_wv, sa_wo, sa_bo, ca_wq, ca_wk, ca_wv, ca_wo, ca_bo, ff_w1, ff_b1, ff_w2, ff_b2):
        import jax, jax.numpy as jnp
        import numpy as np
        D_MODEL = 256
        D_COND = 192
        N_HEADS = 16
        D_HEAD = 64
        D_ATTN = N_HEADS * D_HEAD
        D_FF = 4 * D_MODEL

        def _layernorm(x, g, b, eps=1e-05):
            mu = jnp.mean(x, axis=-1, keepdims=True)
            var = jnp.var(x, axis=-1, keepdims=True)
            return (x - mu) * jax.lax.rsqrt(var + eps) * g + b

        def _attention(xq, xkv, wq, wk, wv, wo, bo):
            B, S, _ = xq.shape
            T = xkv.shape[1]
            q = (xq @ wq).reshape(B, S, N_HEADS, D_HEAD)
            k = (xkv @ wk).reshape(B, T, N_HEADS, D_HEAD)
            v = (xkv @ wv).reshape(B, T, N_HEADS, D_HEAD)
            scale = D_HEAD ** (-0.5)
            attn = jnp.einsum('bihd,bjhd->bhij', q, k) * scale
            attn = jax.nn.softmax(attn, axis=-1)
            out = jnp.einsum('bhij,bjhd->bihd', attn, v).reshape(B, S, D_ATTN)
            return out @ wo + bo
        h = _layernorm(x, ln1_g, ln1_b)
        x = _attention(h, h, sa_wq, sa_wk, sa_wv, sa_wo, sa_bo) + x
        h = _layernorm(x, ln2_g, ln2_b)
        x = _attention(h, cond_emb, ca_wq, ca_wk, ca_wv, ca_wo, ca_bo) + x
        h = _layernorm(x, ln3_g, ln3_b)
        p = h @ ff_w1 + ff_b1
        a, gate = (p[..., :D_FF], p[..., D_FF:])
        h = a * jax.nn.gelu(gate, approximate=False) @ ff_w2 + ff_b2
        return h + x
    x = _L0_xattn_ref(x, ctx_768, L0_xattn_wq1, L0_xattn_wk1, L0_xattn_wv1, L0_xattn_wo1, L0_xattn_bo1, L0_xattn_wq2, L0_xattn_wk2, L0_xattn_wv2, L0_xattn_wo2, L0_xattn_bo2, L0_xattn_w_ff1, L0_xattn_b_ff1, L0_xattn_w_ff2, L0_xattn_b_ff2, L0_xattn_g1, L0_xattn_b1, L0_xattn_g2, L0_xattn_b2, L0_xattn_g3, L0_xattn_b3)
    x = _L1_xattn_ref(x, ctx_768, L1_xattn_ln1_g, L1_xattn_ln1_b, L1_xattn_ln2_g, L1_xattn_ln2_b, L1_xattn_ln3_g, L1_xattn_ln3_b, L1_xattn_sa_wq, L1_xattn_sa_wk, L1_xattn_sa_wv, L1_xattn_sa_wo, L1_xattn_sa_bo, L1_xattn_ca_wq, L1_xattn_ca_wk, L1_xattn_ca_wv, L1_xattn_ca_wo, L1_xattn_ca_bo, L1_xattn_ff_w1, L1_xattn_ff_b1, L1_xattn_ff_w2, L1_xattn_ff_b2)
    return x

_drawn_inputs = setup_inputs


def setup_inputs(seed=0):
    import zlib

    import numpy as np

    out = dict(_drawn_inputs(seed))
    spreads = {'L0_xattn_bo1': (0.0, 0.1),
     'L0_xattn_bo2': (0.0, 0.1),
     'L0_xattn_b_ff1': (0.0, 0.49),
     'L0_xattn_b_ff2': (0.0, 0.1),
     'L0_xattn_g1': (1.0, 0.6),
     'L0_xattn_b1': (0.0, 0.347),
     'L0_xattn_g2': (1.0, 0.6),
     'L0_xattn_b2': (0.0, 0.8),
     'L0_xattn_g3': (1.0, 0.6),
     'L0_xattn_b3': (0.0, 0.8),
     'L1_xattn_ln1_g': (1.0, 0.2),
     'L1_xattn_ln1_b': (0.0, 0.1),
     'L1_xattn_ln2_g': (1.0, 0.2),
     'L1_xattn_ln2_b': (0.0, 0.386),
     'L1_xattn_ln3_g': (1.0, 0.2),
     'L1_xattn_ln3_b': (0.0, 0.1),
     'L1_xattn_sa_bo': (0.0, 0.1),
     'L1_xattn_ca_bo': (0.0, 0.1),
     'L1_xattn_ff_b1': (0.0, 0.1),
     'L1_xattn_ff_b2': (0.0, 0.1)}
    factors = {'L0_xattn_wq1': 8.0, 'L0_xattn_wk1': 8.0, 'L0_xattn_wq2': 8.0, 'L0_xattn_wk2': 8.0}
    for name, (base, spread) in spreads.items():
        noise = np.random.default_rng([zlib.crc32(name.encode()), seed]).standard_normal(out[name].shape)
        drawn = base * np.exp(spread * noise) if base else spread * noise
        out[name] = jnp.asarray(drawn.astype(out[name].dtype))
    for name, factor in factors.items():
        out[name] = (out[name] * factor).astype(out[name].dtype)
    return out
```

```python
import collections
from contextlib import ExitStack, contextmanager

import numpy as np

import concourse.bass as bass
from concourse import mybir
from concourse.alu_op_type import AluOpType as ALU

F32 = mybir.dt.float32
F16 = mybir.dt.float16
ACT = mybir.ActivationFunctionType
AX = mybir.AxisListType

P = 128
BATCH, TOKENS, DIM = 2, 1024, 256
LAYERS = 2
HEADS, DH = 16, 64
INNER = HEADS * DH
CTX, CTX_DIM = 77, 192
FF = 4 * DIM
EPS = 1e-5

PAIRS = HEADS // 2
TILES = TOKENS // P
KC = DIM // P
BLK = 512
BLKS = TOKENS // BLK
W_SCALE = 64.0
W_BACK = 1.0 / W_SCALE
Q_BACK = W_BACK * DH ** -0.5
VW = 2 * DH + 1
OUT_W = DH + 1
HALF = TILES // 2
PIECE = 1024
PAIR_DMAS = 12
FF_CHUNKS = FF // P

Step = collections.namedtuple("Step", "kind step par head ahead")
WORK = ("q", "k", "v", "max", "shift", "merge")
HIGH = ("q", "k", "v", "merge")


class Shape:

    def __init__(self, name, key_tiles, key_rows, ring):
        self.name, self.key_tiles, self.key_rows, self.ring = name, key_tiles, key_rows, ring
        self.own = key_tiles > 1
        self.keys = key_tiles * key_rows
        self.k_blocks = BLKS if self.own else 1
        self.v_blocks = 2 if self.own else 1

    def project(self, par, ahead):
        s = [Step("start", 0, par, 0, ahead)]
        s += [Step("q", b, par, 0, ahead) for b in range(BLKS)]
        s += [Step("k", b, par, 0, ahead) for b in range(self.k_blocks)]
        s += [Step("v", b, par, 0, ahead) for b in range(self.v_blocks)]
        return s

    def maxima(self, par, head):
        first = [Step("arrive", 0, par, 0, 0)] if head == 0 else []
        if self.own:
            tiles = [[Step("max", (t, h), par, head, 0) for h in range(BLKS)] for t in range(TILES)]
        else:
            tiles = [[Step("max", (h, 0), par, head, 0)] for h in range(2)]
        tiles[0] = first + tiles[0]
        tiles[-1] = tiles[-1] + [Step("combine", 0, par, head, 0)]
        return tiles

    def unit(self, par, head, before, after, project, merge):
        kt = self.key_tiles
        nxt = (par, 1) if head == 0 else (1 - par, 0)
        prv = (par, 0) if head == 1 else (1 - par, 1)
        maxima = self.maxima(*nxt) if after else []
        shift = [Step("shift", 0, *nxt, 0)] if after else []
        extra = self.project(1 - par, 1) if project else []
        merging = [Step("merge", h, 1 - par, 0, -1) for h in range(2)] if merge else []
        out = [Step("unit", 0, par, head, 0)]
        if self.own:
            per = [2, 1, 2, 1, 1, 1, 0, 0]
            for s in range(kt):
                out.append(Step("score", s, par, head, 0))
                for _ in range(per[s]):
                    if maxima:
                        out += maxima.pop(0)
                if s >= 1:
                    out.append(Step("refine", s - 1, par, head, 0))
                elif before:
                    out.append(Step("refine", kt - 1, *prv, 0))
                if s >= 2:
                    out.append(Step("value", s - 2, par, head, 0))
                elif before:
                    out.append(Step("value", kt - 2 + s, *prv, 0))
                    if s == 1:
                        out.append(Step("gather", 0, *prv, 0))
                if s == 6:
                    out += shift
                if extra:
                    out += extra[:2] if s == 0 else extra[:1]
                    extra = extra[2:] if s == 0 else extra[1:]
                if s in (3, 4) and merging:
                    out.append(merging.pop(0))
        else:
            for group in maxima:
                out += group
            out.append(Step("score", 0, par, head, 0))
            if before:
                out += [Step("value", 0, *prv, 0), Step("gather", 0, *prv, 0)]
            out += shift
            out += extra
            out += merging
            out.append(Step("refine", 0, par, head, 0))
        return out

    def tail(self, par):
        kt = self.key_tiles
        out = []
        if self.own:
            out += [Step("refine", kt - 1, par, 1, 0)]
            out += [Step("value", kt - 2, par, 1, 0)]
        out += [Step("value", kt - 1, par, 1, 0), Step("gather", 0, par, 1, 0)]
        return out + [Step("merge", h, par, 0, 0) for h in range(2)]

    def pair(self, par, first=False, last=False):
        return (self.unit(par, 0, not first, True, not last, False)
                + self.unit(par, 1, True, not last, False, not first))

    def sections(self):
        head = self.project(0, 0) + sum(self.maxima(0, 0), []) + [Step("shift", 0, 0, 0, 0)]
        last = (PAIRS - 1) % 2
        return [(head, 0, 0), (self.pair(0, first=True), 0, 0),
                (self.pair(1) + self.pair(0), 1, (PAIRS - 2) // 2),
                (self.pair(last, last=True) + self.tail(last), PAIRS - 1, 0)]


SELF = Shape("self", TILES, P, 4)
CROSS = Shape("cross", 1, CTX, 2)


class Pace:

    def __init__(self, shape, phase_round):
        self.sections = shape.sections()
        self.round = phase_round
        self.all = collections.Counter()
        for steps, _, turns in self.sections:
            for s in steps:
                self.all[s.kind] += max(turns, 1)
        self.passed = collections.Counter()
        self.turn = collections.Counter()
        self.base = {}
        self.r = None

    def walk(self, engine, do):
        for steps, pair, turns in self.sections:
            self.turn = collections.Counter(s.kind for s in steps)
            if turns:
                with engine.Fori(0, turns) as r:
                    self.r, self.base = r, {}
                    self._steps(engine, steps, do, pair, r)
                for k in self.turn:
                    self.passed[k] += self.turn[k] * (turns - 1)
            else:
                self.r, self.base = None, {}
                self._steps(engine, steps, do, pair, None)
        self.r, self.base = None, {}

    def _steps(self, engine, steps, do, pair, r):
        self.engine = engine
        at, units = pair, 0
        for s in steps:
            if s.kind == "unit":
                at, units = pair + units // 2, units + 1
            where = at + s.ahead
            do(s, where if r is None else r * 2 + where)
            self.passed[s.kind] += 1

    def here(self, *kinds):
        return sum(self.passed[k] for k in kinds)

    def n(self, *kinds):
        if kinds not in self.base:
            base = self.round * sum(self.all[k] for k in kinds)
            if self.r is not None:
                base = base + self.r * sum(self.turn[k] for k in kinds)
            self.base[kinds] = self.engine.snap(base)
        return self.base[kinds] + self.here(*kinds)


def build(nc, io):
    ctx = ExitStack()
    with ctx:
        def sb(name, shape, dtype=F32):
            return ctx.enter_context(nc.sbuf_tensor(name, shape, dtype))

        def ps(name, columns):
            return ctx.enter_context(nc.psum_tensor(name, [P, columns], F32))

        def sem(name):
            return ctx.enter_context(nc.semaphore(name))

        scores = [ps(f"scores{i}", 2 * BLK) for i in range(2)]
        outs = [ps(f"outs{i}", BLK) for i in range(2)]
        work = [ps(f"work{i}", BLK) for i in range(2)]
        four = [scores[i][:, h * BLK:(h + 1) * BLK] for i in range(2) for h in range(2)]

        ident = sb("ident", [P, P])
        ident16 = sb("ident16", [P, P], F16)
        x = sb("x_sb", [P, TILES, DIM])
        xn = sb("xn", [P, 4, DIM])
        stats = sb("stats", [P, TILES, 6])
        mean_var = sb("mean_var", [P, TILES, 2])
        var_eps = sb("var_eps", [P, TILES])
        rstd = sb("rstd", [P, TILES])
        eps = sb("eps", [P, 2])
        minus_half = sb("minus_half", [P, 2])
        t32 = sb("t32", [P, 2, KC, 2 * P])
        hT = [sb(f"hT{i}", [P, KC, TOKENS], F16) for i in range(2)]
        cT = [sb(f"cT{i}", [P, 2, CTX], F16) for i in range(2)]
        ctx_sb = sb("ctx_sb", [CTX, CTX_DIM])
        n_par = 6 * KC + 2 * FF_CHUNKS
        params = sb("params", [P, n_par])
        bias_a = sb("bias_a", [P, FF_CHUNKS])
        rows = sb("rows", [P, 3, DIM])
        raw = sb("raw", [P, PIECE])
        wp = [sb(f"wp{i}", [P, 2, 6, P], F16) for i in range(2)]
        wo = [sb(f"wo{i}", [P, PAIRS, DIM], F16) for i in range(2)]
        w1 = [sb(f"w1{i}", [P, KC, 2 * FF], F16) for i in range(2)]
        w2 = [sb(f"w2{i}", [P, FF_CHUNKS, DIM], F16) for i in range(2)]
        staged = [[sb(f"staged_{a}{i}", [P, TOKENS], F16) for i in range(2)] for a in "qk"]
        qa = [[sb(f"qa{p}{i}", [P, TOKENS], F16) for i in range(2)] for p in range(2)]
        qb = [[sb(f"qb{p}{i}", [P, TOKENS], F16) for i in range(2)] for p in range(2)]
        ka = [[sb(f"ka{p}{i}", [P, TOKENS], F16) for i in range(2)] for p in range(2)]
        kb = [[sb(f"kb{p}{i}", [P, TOKENS], F16) for i in range(2)] for p in range(2)]
        vals = [sb(f"vals{p}", [P, TILES, 2, VW], F16) for p in range(2)]
        prob32 = sb("prob32", [P, 2, TOKENS])
        prob = [sb(f"prob{i}", [P, 4, TOKENS], F16) for i in range(2)]
        minima = sb("minima", [P, TILES, 2])
        shift16 = sb("shift16", [P, TILES], F16)
        shift_rows = sb("shift_rows", [TILES, P], F16)
        inv = sb("inv", [P, TILES])
        o_nat = sb("o_nat", [P, 2, TILES, P])
        oT = [sb(f"oT{i}", [P, PAIRS, TOKENS], F16) for i in range(2)]
        gelu32 = prob32[:, :, 0:BLK]
        inner32 = prob32[:, :, BLK:2 * BLK]

        consts_ready = sem("consts_ready")
        ones_ready = sem("ones_ready")
        x_loaded = sem("x_loaded")
        ctx_loaded = sem("ctx_loaded")
        params_loaded = sem("params_loaded")
        ctx_turned = sem("ctx_turned")
        ctx_high = sem("ctx_high")
        ctx_split = sem("ctx_split")
        phase_over = sem("phase_over")
        raw_loaded = sem("raw_loaded")
        raw_scaled = sem("raw_scaled")
        weights_split = sem("weights_split")
        pair_projected = sem("pair_projected")
        y_full = sem("y_full")
        y_free = sem("y_free")
        moments_ready = sem("moments_ready")
        centred = sem("centred")
        var_ready = sem("var_ready")
        rstd_ready = sem("rstd_ready")
        norm_ready = sem("norm_ready")
        turned_full = sem("turned_full")
        turned_out = sem("turned_out")
        norm_split = sem("norm_split")
        bias_added = sem("bias_added")
        A = {}
        for s in (SELF, CROSS):
            names = ("work_full work_high work_free scores_full exp_done probs_low probs_used "
                     "outs_free inverse_ready heads_ready shift_combined row_ready")
            A[s.name] = collections.namedtuple("Sems", names)(*[sem(f"{s.name}_{n}") for n in names.split()])
        bias_ready = sem("bias_ready")
        up_full = sem("up_full")
        gelu_ready = sem("gelu_ready")
        inner_ready = sem("inner_ready")
        inner_high = sem("inner_high")
        inner_low = sem("inner_low")
        x_stored = sem("x_stored")

        PHASES = 7
        CREDIT = 1
        held = sem("held")
        block = ctx.enter_context(nc.Block())

        def hold(eng, sem_, value):
            eng.wait_ge(sem_, value)
            eng.sem_inc(held, 1)

        def end_phase(eng, g, index):
            eng.drain().then_inc(phase_over, 1)
            hold(eng, phase_over, g * (3 * PHASES) + (3 * (index + 1) + CREDIT))

        @block.sync
        def _(sp):
            def attention(shape, g):
                a, pace = A[shape.name], Pace(shape, g)
                tiles = 2 * shape.key_tiles

                def spread(which, dests, step):
                    hold(sp, a.work_free, pace.n(*WORK) + 3)
                    if step.ahead:
                        sp.wait_ge(a.scores_full, (pace.n("start") - 2) * tiles + CREDIT)
                    n = TOKENS if which == 0 else shape.keys
                    for head in range(2):
                        for dest, row, part in dests:
                            sp.dma_start(dest[step.par][head][row:row + DH, 0:n],
                                         staged[which][part][head * DH:(head + 1) * DH, 0:n])\
                              .then_inc(a.heads_ready, 16)

                def do(step, pair):
                    if step.kind == "q" and step.step == BLKS - 1:
                        spread(0, [(qa, 0, 0), (qa, DH, 0), (qb, 0, 1)], step)
                    elif step.kind == "k" and step.step == shape.k_blocks - 1:
                        spread(1, [(ka, 0, 0), (ka, DH, 1), (kb, 0, 0)], step)
                    elif step.kind == "shift":
                        sp.wait_ge(a.work_free, pace.n(*WORK) + 3)
                        sp.dma_start(qb[step.par][step.head][DH:DH + 1, :]
                                     .rearrange("o (t c) -> o t c", t=TILES),
                                     shift_rows[:, :]).then_inc(a.row_ready, 16)

                pace.walk(sp, do)

            sp.sem_inc(x_stored, CREDIT)
            for a in A.values():
                sp.sem_inc(a.heads_ready, CREDIT)
                sp.sem_inc(a.row_ready, CREDIT)
            with sp.Fori(0, BATCH) as b:
                sp.wait_ge(x_stored, b * 16 + CREDIT)
                sp.dma_start(x[:, :, :], io["x"][bass.ds(b, 1), :, :]
                             .rearrange("o (t p) d -> p (o t) d", p=P)).then_inc(x_loaded, 16)
                sp.dma_start(ctx_sb[:, :], io["ctx"][bass.ds(b, 1), :, :]
                             .rearrange("o t d -> (o t) d")).then_inc(ctx_loaded, 16)
                with sp.Fori(0, LAYERS) as l:
                    g = sp.snap(b * LAYERS + l)
                    hold(sp, phase_over, g * (3 * PHASES) + CREDIT)
                    hold(sp, bias_added, g * 3 + CREDIT)
                    sp.dma_start(params[:, :], io["params"][bass.ds(l, 1), :, :]
                                 .rearrange("o p n -> (o p) n")).then_inc(params_loaded, 16)
                    sp.dma_start(rows[:, :, :], io["rows"][bass.ds(l, 1), :, :]
                                 .to_broadcast([P, 3, DIM])).then_inc(params_loaded, 16)
                    attention(SELF, g)
                    attention(CROSS, g)
                sp.wait_ge(phase_over, (b + 1) * (3 * PHASES * LAYERS) + CREDIT)
                sp.dma_start(io["out"][bass.ds(b, 1), :, :].rearrange("o (t p) d -> p (o t) d", p=P),
                             x[:, :, :]).then_inc(x_stored, 16)
            sp.wait_ge(x_stored, BATCH * 16 + CREDIT)

        @block.gpsimd
        def _(pool):
            pool.memset(ident[:, :], 0.0).then_inc(consts_ready, 1)
            pool.memset(eps[:, :], EPS).then_inc(consts_ready, 1)
            pool.memset(minus_half[:, :], -0.5).then_inc(consts_ready, 1)
            pool.wait_ge(consts_ready, 3)
            pool.affine_select(out=ident[:, :], in_=ident[:, :], compare_op=ALU.not_equal, fill=1.0,
                               base=0, pattern=[[-1, P]], channel_multiplier=1).then_inc(consts_ready, 1)
            pool.wait_ge(consts_ready, 4)
            pool.tensor_copy(ident16[:, :], ident[:, :]).then_inc(consts_ready, 1)

            def load(at, moves):
                hold(pool, weights_split, at[1] + CREDIT)
                for dest, source in moves:
                    pool.dma_start(dest, source).then_inc(raw_loaded, 16)
                hold(pool, raw_loaded, (at[0] + len(moves)) * 16)
                return at[0] + len(moves), at[1]

            def split(at, source, high, low):
                pool.tensor_scalar(high, source, W_SCALE, 1.0, ALU.mult, ALU.mult)
                pool.tensor_scalar(source, source, W_SCALE, 1.0, ALU.mult, ALU.mult)\
                    .then_inc(raw_scaled, 1)
                pool.wait_ge(raw_scaled, at[1] + 1)
                pool.tensor_tensor(low, source, high, ALU.subtract).then_inc(weights_split, 1)
                return at[0], at[1] + 1

            def self_pair(at, l, pair, par, number):
                pool.wait_ge(pair_projected, number + 1)
                cut = raw[:, 0:6 * P].rearrange("p (s n) -> p s n", s=6)
                moves = []
                for name, first, step in (("wq1", 0, 1), ("wk1", 2, 2), ("wv1", 3, 2)):
                    source = io[name][bass.ds(l, 1), :, bass.ds(pair * P, P)]
                    moves.append((cut[:, first:first + step + 1:step, :],
                                  source.rearrange("o (c p) n -> p (o c) n", p=P)))
                at = load(at, moves)
                return split(at, cut, wp[par][:, 0, :, :], wp[par][:, 1, :, :])

            def cross_pair(at, l, pair, par, number):
                pool.wait_ge(pair_projected, number + 1)
                cut = raw[:, 0:6 * P].rearrange("p (s n) -> p s n", s=6)
                rest = CTX_DIM - P
                moves = [(cut[:, 0:2, :], io["wq2"][bass.ds(l, 1), :, bass.ds(pair * P, P)]
                          .rearrange("o (c p) n -> p (o c) n", p=P))]
                for n, name in enumerate(("wk2", "wv2")):
                    w = io[name]
                    moves.append((cut[:, 2 + n, :], w[bass.ds(l, 1), 0:P, bass.ds(pair * P, P)]
                                  .rearrange("o p n -> (o p) n")))
                    moves.append((cut[0:rest, 4 + n, :], w[bass.ds(l, 1), P:CTX_DIM, bass.ds(pair * P, P)]
                                  .rearrange("o p n -> (o p) n")))
                at = load(at, moves)
                at = split(at, cut[:, 0:4, :], wp[par][:, 0, 0:4, :], wp[par][:, 1, 0:4, :])
                return split(at, cut[0:rest, 4:6, :], wp[par][0:rest, 0, 4:6, :],
                             wp[par][0:rest, 1, 4:6, :])

            def pairs(at, one, l, number):
                before = at
                per = PER_PAIR[one.__name__]
                with pool.Fori(0, (PAIRS - 2) // 2) as r:
                    at = (pool.snap(before[0] + r * (2 * per[0])), pool.snap(before[1] + r * (2 * per[1])))
                    before_them = pool.snap(number + r * 2)
                    for par in range(2):
                        at = one(at, l, r * 2 + (2 + par), par, before_them + (2 + par))
                return (before[0] + (PAIRS - 2) * per[0], before[1] + (PAIRS - 2) * per[1])

            def narrow(at, l, name, dest):
                half = PIECE // DIM
                for c in range(0, PAIRS, half):
                    cut = raw[:, :].rearrange("p (c n) -> p c n", n=DIM)
                    at = load(at, [(cut, io[name][bass.ds(l, 1), c * P:(c + half) * P, :]
                                    .rearrange("o (c p) n -> p (o c) n", p=P))])
                    at = split(at, cut, dest[0][:, c:c + half, :], dest[1][:, c:c + half, :])
                return at

            def wide(at, l):
                for c in range(KC):
                    for n in range(0, 2 * FF, PIECE):
                        at = load(at, [(raw[:, :], io["w1"][bass.ds(l, 1), c * P:(c + 1) * P, n:n + PIECE]
                                        .rearrange("o p n -> (o p) n"))])
                        at = split(at, raw[:, :], w1[0][:, c, n:n + PIECE], w1[1][:, c, n:n + PIECE])
                return at

            def norm(index):
                for p in range(TILES // 2):
                    two = slice(2 * p, 2 * p + 2)
                    pool.wait_ge(moments_ready, index * TILES + 2 * (p + 1))
                    pool.tensor_tensor(var_eps[:, two], mean_var[:, two, 1], eps[:, :], ALU.add)\
                        .then_inc(var_ready, 1)
                    pool.wait_ge(var_ready, index * (TILES // 2) + (p + 1))
                    pool.tensor_tensor(rstd[:, two], var_eps[:, two], minus_half[:, :], ALU.pow)\
                        .then_inc(rstd_ready, 1)

            def add_bias(index, row):
                pool.wait_ge(norm_ready, index * TILES + TILES)
                pool.tensor_tensor(x[:, :, :], x[:, :, :],
                                   rows[:, row, :].unsqueeze(1).to_broadcast([P, TILES, DIM]), ALU.add)\
                    .then_inc(bias_added, 1)

            pool.sem_inc(weights_split, CREDIT)
            pool.sem_inc(bias_added, CREDIT)
            with pool.Fori(0, BATCH) as b:
                with pool.Fori(0, LAYERS) as l:
                    g = pool.snap(b * LAYERS + l)
                    at = (pool.snap(g * DMAS), pool.snap(g * SPLITS))
                    number = pool.snap(g * (2 * PAIRS))
                    at = self_pair(at, l, 0, 0, number)
                    at = self_pair(at, l, 1, 1, number + 1)
                    norm(pool.snap(g * 3))
                    pool.wait_ge(params_loaded, (g + 1) * 32)
                    add_bias(pool.snap(g * 3), 0)
                    at = pairs(at, self_pair, l, number)
                    pool.wait_ge(phase_over, g * (3 * PHASES) + CREDIT)
                    at = narrow(at, l, "wo1", wo)
                    at = wide(at, l)
                    at = narrow(at, l, "w2", w2)
                    at = cross_pair(at, l, 0, 0, number + PAIRS)
                    at = cross_pair(at, l, 1, 1, number + (PAIRS + 1))
                    norm(pool.snap(g * 3 + 1))
                    add_bias(pool.snap(g * 3 + 1), 1)
                    at = pairs(at, cross_pair, l, pool.snap(number + PAIRS))
                    pool.wait_ge(phase_over, g * (3 * PHASES) + (3 * 3 + CREDIT))
                    at = narrow(at, l, "wo2", wo)
                    norm(pool.snap(g * 3 + 2))
                    add_bias(pool.snap(g * 3 + 2), 2)

        @block.tensor
        def _(pe):
            pe.sem_inc(pair_projected, 2)
            for a in A.values():
                pe.sem_inc(a.scores_full, CREDIT)
            pe.sem_inc(A["self"].probs_used, SELF.ring)
            pe.sem_inc(A["cross"].probs_used, CROSS.ring)

            def three(out, left, right, first, last):
                pe.matmul(out, left[0], right[0], start=first, stop=False)
                pe.matmul(out, left[0], right[1], start=False, stop=False)
                return pe.matmul(out, left[1], right[0], start=False, stop=last)

            def attention(shape, g):
                a, pace = A[shape.name], Pace(shape, g)
                kr, kt = shape.key_rows, shape.key_tiles
                ctx_rows = (P, CTX_DIM - P)
                projected = []

                def bank():
                    pe.wait_ge(a.work_free, pace.n(*WORK) + 1)
                    return work[pace.here(*WORK) % 2]

                def weight(par, c, column, k=P):
                    return [wp[par][0:k, part, column + (c if column == 0 else 2 * c), :] for part in range(2)]

                def keys_in(c, cols, k=P):
                    source = hT if shape.own else cT
                    return [source[part][0:k, c, cols] for part in range(2)]

                def do(step, pair):
                    par, head, s = step.par, step.head, step.step
                    if step.kind == "start":
                        before = (pace.n("start") + 1) if shape.own else pace.n("start") * 2
                        start = pe.snap(g * (SPLITS - PAIRS * (1 if shape.own else 2)))
                        pe.wait_ge(weights_split, start + (before if shape.own else before + (2 * PAIRS + 2)) + CREDIT)
                    elif step.kind == "q":
                        out = bank()
                        for c in range(KC):
                            last = three(out[:, :], weight(par, c, 0),
                                         [hT[part][:, c, s * BLK:(s + 1) * BLK] for part in range(2)],
                                         c == 0, c == KC - 1)
                        last.then_inc(a.work_full, 1)
                    elif step.kind == "k":
                        out = bank()
                        n = min(BLK, shape.keys)
                        for c in range(2):
                            k = P if shape.own else ctx_rows[c]
                            last = three(out[:, 0:n], weight(par, c, 2, k),
                                         keys_in(c, slice(s * BLK, s * BLK + n), k), c == 0, c == 1)
                        last.then_inc(a.work_full, 1)
                    elif step.kind == "v":
                        out = bank()
                        for i in range(4 if shape.own else 1):
                            t = 4 * s + i
                            for c in range(2):
                                k = P if shape.own else ctx_rows[c]
                                last = three(out[0:kr, i * P:(i + 1) * P],
                                             keys_in(c, slice(t * kr, (t + 1) * kr), k),
                                             weight(par, c, 3, k), c == 0, c == 1)
                        last.then_inc(a.work_full, 1)
                        projected.append(step)
                    elif step.kind == "arrive":
                        pe.wait_ge(a.heads_ready, (pace.n("arrive") + 1) * (16 * PAIR_DMAS) + CREDIT)
                    elif step.kind == "max":
                        out = bank()
                        if shape.own:
                            t, h = s
                            last = pe.matmul(out[:, :], qa[par][head][:, t * P:(t + 1) * P],
                                             ka[par][head][:, h * BLK:(h + 1) * BLK], start=True, stop=True)
                        else:
                            for i in range(4):
                                t = 4 * s[0] + i
                                last = pe.matmul(out[:, i * CTX:(i + 1) * CTX],
                                                 qa[par][head][:, t * P:(t + 1) * P],
                                                 ka[par][head][:, 0:CTX], start=True, stop=True)
                        last.then_inc(a.work_full, 1)
                    elif step.kind == "shift":
                        out = bank()
                        pe.wait_ge(a.shift_combined, pace.n("shift") + 1)
                        pe.transpose(out[0:TILES, 0:P // 2].bitcast(F16), shift16[:, :], ident16[:, :])\
                          .then_inc(a.work_full, 1)
                    elif step.kind == "unit":
                        pe.wait_ge(a.row_ready, (pace.n("unit") + 1) * 16 + CREDIT)
                    elif step.kind == "score":
                        pe.wait_ge(a.exp_done, pace.n("score") + 1)
                        out = scores[pace.here("score") % 2]
                        cols = slice(s * kr, (s + 1) * kr)
                        for h in range(BLKS):
                            q = slice(h * BLK, (h + 1) * BLK)
                            last = pe.matmul(out[0:kr, q], ka[par][head][:, cols],
                                             qa[par][head][:, q], start=True, stop=False)
                            if s == 0 and projected:
                                last.then_inc(pair_projected, 1)
                                projected.clear()
                        for h in range(BLKS):
                            q = slice(h * BLK, (h + 1) * BLK)
                            last = pe.matmul(out[0:kr, q], kb[par][head][0:DH + 1, cols],
                                             qb[par][head][0:DH + 1, q], start=False, stop=True)
                        last.then_inc(a.scores_full, 1)
                    elif step.kind == "value":
                        slot = pace.here("value") % shape.ring
                        pe.wait_ge(a.probs_low, pace.n("value") + 3)
                        if s == 0:
                            pe.wait_ge(a.outs_free, pace.n("gather") * 2 + 2)
                        for t in range(TILES):
                            out = outs[t // HALF][:, (t % HALF) * OUT_W:(t % HALF + 1) * OUT_W]
                            p_hi, p_lo = [prob[i][0:kr, slot, t * P:(t + 1) * P] for i in range(2)]
                            v = vals[par][0:kr, s, head, :]
                            pe.matmul(out, p_hi, v[:, DH:VW], start=(s == 0 and t % HALF == 0),
                                      stop=False, skip_group_check=True)
                            pe.matmul(out[:, 0:DH], p_hi, v[:, 0:DH], start=False, stop=False,
                                      skip_group_check=True)
                            last = pe.matmul(out, p_lo, v[:, DH:VW], start=False,
                                             stop=(s == kt - 1), skip_group_check=True)
                        last.then_inc(a.probs_used, 1)
                    elif step.kind == "merge":
                        out = bank()
                        pe.wait_ge(a.outs_free, pace.n("merge") * 2 + (6 if s == 0 else 4))
                        for i in range(HALF):
                            last = pe.transpose(out[:, i * P:(i + 1) * P], o_nat[:, par, s * HALF + i, :],
                                                ident[:, :])
                        last.then_inc(a.work_full, 1)

                pace.walk(pe, do)

            def project(index, t, w):
                out = four[t % 2][:, 0:DIM]
                pe.wait_ge(y_free, index * TILES + (t + 1))
                for c in range(PAIRS):
                    last = three(out, [oT[part][:, c, t * P:(t + 1) * P] for part in range(2)],
                                 [w[part][:, c, :] for part in range(2)], c == 0, c == PAIRS - 1)
                last.then_inc(y_full, 1)

            def turn(index, p):
                pe.wait_ge(norm_ready, index * TILES + 2 * (p + 1))
                if p >= 2:
                    pe.wait_ge(turned_out, index * (TILES // 2) + (p - 1))
                for c in range(KC):
                    for i in range(2):
                        last = pe.transpose(work[p % 2][:, (2 * c + i) * P:(2 * c + i + 1) * P],
                                            xn[:, (2 * p + i) % 4, c * P:(c + 1) * P], ident[:, :])
                last.then_inc(turned_full, 1)

            def project_and_turn(g, k, w, splits, norm_index):
                index = pe.snap(g * 3 + k)
                pe.wait_ge(weights_split, g * SPLITS + (splits + CREDIT))
                for p in range(TILES // 2):
                    project(index, 2 * p, w)
                    project(index, 2 * p + 1, w)
                    if norm_index is not None and p >= 2:
                        turn(norm_index, p - 2)
                if norm_index is not None:
                    turn(norm_index, TILES // 2 - 2)
                    turn(norm_index, TILES // 2 - 1)

            def up(g):
                pe.wait_ge(weights_split, g * SPLITS + (PAIRS + 2 + 4 + CREDIT))
                base = pe.snap(g * (BLKS * FF_CHUNKS))
                for n in range(BLKS * FF_CHUNKS):
                    m, s = divmod(n, BLKS)
                    pe.wait_ge(inner_ready, base + (n + 1))
                    for half in (1, 0):
                        out = four[2 * (n % 2) + half]
                        col = slice(half * FF + m * P, half * FF + (m + 1) * P)
                        for c in range(KC):
                            last = three(out, [w1[part][:, c, col] for part in range(2)],
                                         [hT[part][:, c, s * BLK:(s + 1) * BLK] for part in range(2)],
                                         c == 0, c == KC - 1)
                    last.then_inc(up_full, 1)

            pe.wait_ge(consts_ready, 5)
            pe.wait_ge(ones_ready, 1)
            with pe.Fori(0, BATCH) as b:
                pe.wait_ge(ctx_loaded, (b + 1) * 16)
                pe.transpose(work[0][:, 0:CTX], ctx_sb[:, 0:P], ident[0:CTX, 0:CTX])
                pe.transpose(work[0][0:CTX_DIM - P, P:P + CTX], ctx_sb[:, P:CTX_DIM],
                             ident[0:CTX, 0:CTX]).then_inc(ctx_turned, 1)
                hold(pe, ctx_split, b + 1)
                with pe.Fori(0, LAYERS) as l:
                    g = pe.snap(b * LAYERS + l)
                    for p in range(TILES // 2):
                        turn(pe.snap(g * 3), p)
                    end_phase(pe, g, 0)
                    attention(SELF, g)
                    end_phase(pe, g, 1)
                    project_and_turn(g, 0, wo, PAIRS + 2, pe.snap(g * 3 + 1))
                    end_phase(pe, g, 2)
                    attention(CROSS, g)
                    end_phase(pe, g, 3)
                    project_and_turn(g, 1, wo, SPLITS, pe.snap(g * 3 + 2))
                    end_phase(pe, g, 4)
                    up(g)
                    end_phase(pe, g, 5)
                    project_and_turn(g, 2, w2, PAIRS + 2 + 4 + 2, None)
                    end_phase(pe, g, 6)

        @block.scalar
        def _(act):
            act.sem_inc(A["self"].exp_done, 2)
            act.sem_inc(A["cross"].exp_done, 2)

            def attention(shape, g):
                a, pace = A[shape.name], Pace(shape, g)
                kr, kt = shape.key_rows, shape.key_tiles

                def bank():
                    act.wait_ge(a.work_full, pace.n(*WORK) + 1)
                    return work[pace.here(*WORK) % 2]

                def do(step, pair):
                    par, head, s = step.par, step.head, step.step
                    if step.kind == "start":
                        act.wait_ge(a.heads_ready, pace.n("start") * (16 * PAIR_DMAS) + CREDIT)
                    elif step.kind in "qk":
                        out = bank()
                        n = BLK if step.kind == "q" else min(BLK, shape.keys)
                        act.activation(staged["qk".index(step.kind)][0][:, s * BLK:s * BLK + n], out[:, 0:n],
                                       ACT.Copy, scale=Q_BACK if step.kind == "q" else W_BACK)\
                           .then_inc(a.work_high, 1)
                    elif step.kind == "v":
                        out = bank()
                        tiles = 4 if shape.own else 1
                        if step.ahead and pace.here("start") > 2:
                            act.wait_ge(a.probs_used, (pace.n("start") - 2) * (2 * kt) + shape.ring)
                        act.activation(vals[par][0:kr, tiles * s:tiles * (s + 1), :, DH:2 * DH],
                                       out[0:kr, 0:tiles * P].rearrange("p (t h d) -> p t h d", h=2, d=DH),
                                       ACT.Copy, scale=W_BACK).then_inc(a.work_high, 1)
                    elif step.kind == "merge":
                        out = bank()
                        act.activation(oT[0][:, bass.ds(pair, 1), s * BLK:(s + 1) * BLK]
                                       .rearrange("p o n -> p (o n)"), out[:, :], ACT.Copy)\
                           .then_inc(a.work_high, 1)
                    elif step.kind == "score":
                        n = pace.here("score")
                        source = scores[n % 2][0:kr, :]
                        act.wait_ge(a.scores_full, pace.n("score") + (1 + CREDIT))
                        act.wait_ge(a.probs_low, pace.n("score") + 1)
                        act.activation(prob32[0:kr, n % 2, :], source, ACT.Exp)
                        act.wait_ge(a.probs_used, pace.n("score") + 1)
                        act.activation(prob[0][0:kr, n % shape.ring, :], source, ACT.Exp)\
                           .then_inc(a.exp_done, 1)

                pace.walk(act, do)

            def norm(index, k):
                for p in range(TILES // 2):
                    act.wait_ge(turned_full, index * (TILES // 2) + (p + 1))
                    if p >= 2:
                        act.wait_ge(norm_split, index * (TILES // 2) + (p - 1))
                    for c in range(KC):
                        source = work[p % 2][:, 2 * c * P:2 * (c + 1) * P]
                        gain = params[:, 2 * k * KC + c:2 * k * KC + c + 1]
                        bias = params[:, (2 * k + 1) * KC + c:(2 * k + 1) * KC + c + 1]
                        act.activation(hT[0][:, c, 2 * p * P:2 * (p + 1) * P], source, ACT.Identity,
                                       bias=bias, scale=gain)
                        last = act.activation(t32[:, p % 2, c, :], source, ACT.Identity,
                                              bias=bias, scale=gain)
                    last.then_inc(turned_out, 1)

            def up(g):
                base = act.snap(g * (BLKS * FF_CHUNKS))

                def high(n):
                    m, s = divmod(n, BLKS)
                    act.wait_ge(inner_ready, base + (n + 3))
                    act.activation(oT[0][:, m, s * BLK:(s + 1) * BLK], inner32[:, n % 2, :], ACT.Copy,
                                   scale=W_BACK).then_inc(inner_high, 1)

                for n in range(BLKS * FF_CHUNKS):
                    m = n // BLKS
                    act.wait_ge(up_full, base + (n + 1))
                    act.wait_ge(inner_ready, base + (n + 1))
                    act.activation(gelu32[:, n % 2, :], four[2 * (n % 2) + 1], ACT.Gelu, scale=W_BACK,
                                   bias=params[:, 6 * KC + FF_CHUNKS + m:6 * KC + FF_CHUNKS + m + 1])\
                       .then_inc(gelu_ready, 1)
                    if n:
                        high(n - 1)
                high(BLKS * FF_CHUNKS - 1)

            with act.Fori(0, BATCH) as b:
                act.wait_ge(ctx_turned, b + 1)
                act.activation(cT[0][:, 0, :], work[0][:, 0:CTX], ACT.Copy)
                act.activation(cT[0][0:CTX_DIM - P, 1, :], work[0][0:CTX_DIM - P, P:P + CTX], ACT.Copy)\
                   .then_inc(ctx_high, 1)
                with act.Fori(0, LAYERS) as l:
                    g = act.snap(b * LAYERS + l)
                    act.wait_ge(params_loaded, (g + 1) * 32)
                    norm(act.snap(g * 3), 0)
                    end_phase(act, g, 0)
                    attention(SELF, g)
                    end_phase(act, g, 1)
                    norm(act.snap(g * 3 + 1), 1)
                    end_phase(act, g, 2)
                    attention(CROSS, g)
                    end_phase(act, g, 3)
                    norm(act.snap(g * 3 + 2), 2)
                    end_phase(act, g, 4)
                    up(g)
                    end_phase(act, g, 5)
                    end_phase(act, g, 6)

        @block.vector
        def _(dve):
            for p in range(2):
                for i in range(2):
                    dve.memset(kb[p][i][DH:DH + 1, :], 1.0)
                dve.memset(vals[p][:, :, :, 2 * DH:VW], 1.0)
            dve.drain().then_inc(ones_ready, 1)
            dve.wait_ge(ones_ready, 1)
            dve.sem_inc(y_free, 2)
            dve.sem_inc(phase_over, CREDIT)
            dve.sem_inc(inner_ready, 2)
            for a in A.values():
                dve.sem_inc(a.work_free, 2)
                dve.sem_inc(a.probs_low, 2)
                dve.sem_inc(a.outs_free, 2)

            def attention(shape, g):
                a, pace = A[shape.name], Pace(shape, g)
                kr, kt = shape.key_rows, shape.key_tiles

                def bank():
                    dve.wait_ge(a.work_full, pace.n(*WORK) + 1)
                    return work[pace.here(*WORK) % 2]

                def do(step, pair):
                    par, head, s = step.par, step.head, step.step
                    if step.kind in HIGH:
                        dve.wait_ge(a.work_high, pace.n(*HIGH) + 1)
                        out = work[pace.here(*WORK) % 2]
                    if step.kind in ("q", "k"):
                        n = BLK if step.kind == "q" else min(BLK, shape.keys)
                        parts = staged["qk".index(step.kind)]
                        cols = slice(s * BLK, s * BLK + n)
                        dve.scalar_tensor_tensor(out=parts[1][:, cols], in0=out[:, 0:n],
                                                 scalar=Q_BACK if step.kind == "q" else W_BACK,
                                                 in1=parts[0][:, cols], op0=ALU.mult, op1=ALU.subtract)\
                           .then_inc(a.work_free, 1)
                    elif step.kind == "v":
                        n = 8 if shape.own else 2
                        v = vals[par][0:kr, :, :, :].rearrange("p t h w -> p (t h) w")[:, n * s:n * (s + 1), :]
                        dve.scalar_tensor_tensor(out=v[:, :, 0:DH],
                                                 in0=out[0:kr, 0:n * DH].rearrange("p (n d) -> p n d", d=DH),
                                                 scalar=W_BACK, in1=v[:, :, DH:2 * DH],
                                                 op0=ALU.mult, op1=ALU.subtract).then_inc(a.work_free, 1)
                    elif step.kind == "merge":
                        high, low = [oT[i][:, bass.ds(pair, 1), s * BLK:(s + 1) * BLK]
                                     .rearrange("p o n -> p (o n)") for i in range(2)]
                        dve.tensor_tensor(low, out[:, :], high, ALU.subtract).then_inc(a.work_free, 1)
                    elif step.kind == "max":
                        out = bank()
                        if shape.own:
                            t, h = s
                            dve.tensor_reduce(minima[:, t, h:h + 1], out[:, :], AX.X, ALU.max, negate=True)\
                               .then_inc(a.work_free, 1)
                        else:
                            dve.tensor_reduce(shift16[:, 4 * s[0]:4 * s[0] + 4],
                                              out[:, 0:4 * CTX].rearrange("p (t k) -> p t k", t=4),
                                              AX.X, ALU.max, negate=True).then_inc(a.work_free, 1)
                    elif step.kind == "combine":
                        if shape.own:
                            dve.wait_ge(a.work_free, pace.n(*WORK) + 2)
                            dve.tensor_reduce(shift16[:, :], minima[:, :, :], AX.X, ALU.min)\
                               .then_inc(a.shift_combined, 1)
                        else:
                            dve.wait_ge(a.work_free, pace.n(*WORK) + 2)
                            dve.sem_inc(a.shift_combined, 1)
                    elif step.kind == "shift":
                        out = bank()
                        dve.wait_ge(a.row_ready, pace.n("shift") * 16 + CREDIT)
                        dve.tensor_copy(shift_rows[:, :], out[0:TILES, 0:P // 2].bitcast(F16))\
                           .then_inc(a.work_free, 1)
                    elif step.kind == "refine":
                        n = pace.here("refine")
                        dve.wait_ge(a.exp_done, pace.n("refine") + 3)
                        slot = n % shape.ring
                        dve.tensor_tensor(prob[1][0:kr, slot, :], prob32[0:kr, n % 2, :],
                                          prob[0][0:kr, slot, :], ALU.subtract).then_inc(a.probs_low, 1)
                    elif step.kind == "gather":
                        dve.wait_ge(a.probs_used, pace.n("value") + shape.ring)
                        for h in range(2):
                            view = outs[h][:, 0:HALF * OUT_W].rearrange("p (t w) -> p t w", w=OUT_W)
                            last = dve.reciprocal(inv[:, h * HALF:(h + 1) * HALF], view[:, :, DH])
                        last.then_inc(a.inverse_ready, 1)
                        dve.wait_ge(a.inverse_ready, pace.n("gather") + 1)
                        for h in range(2):
                            view = outs[h][:, 0:HALF * OUT_W].rearrange("p (t w) -> p t w", w=OUT_W)
                            dve.tensor_tensor(
                                o_nat[:, par, h * HALF:(h + 1) * HALF, head * DH:(head + 1) * DH],
                                view[:, :, 0:DH],
                                inv[:, h * HALF:(h + 1) * HALF].unsqueeze(2).to_broadcast([P, HALF, DH]),
                                ALU.mult).then_inc(a.outs_free, 1)

                pace.walk(dve, do)

            def moments(index, p):
                for t in (2 * p, 2 * p + 1):
                    dve.bn_stats(stats[:, t, :], x[:, t, :]).then_inc(centred, 1)
                hold(dve, centred, index * TILES + 2 * (p + 1))
                for t in (2 * p, 2 * p + 1):
                    dve.bn_aggr(mean_var[:, t, :], stats[:, t, :]).then_inc(moments_ready, 1)

            def normalise(index, p):
                dve.wait_ge(rstd_ready, index * (TILES // 2) + (p + 1))
                if p >= 2:
                    dve.wait_ge(turned_full, index * (TILES // 2) + (p - 1))
                for t in (2 * p, 2 * p + 1):
                    dve.tensor_scalar(xn[:, t % 4, :], x[:, t, :], mean_var[:, t, 0:1], rstd[:, t:t + 1],
                                      ALU.subtract, ALU.mult).then_inc(norm_ready, 1)

            def split(index, p):
                dve.wait_ge(turned_out, index * (TILES // 2) + (p + 1))
                cols = slice(2 * p * P, 2 * (p + 1) * P)
                dve.tensor_tensor(hT[1][:, :, cols], t32[:, p % 2, :, :], hT[0][:, :, cols], ALU.subtract)\
                   .then_inc(norm_split, 1)

            def take(index, t):
                dve.wait_ge(y_full, index * TILES + (t + 1))
                dve.scalar_tensor_tensor(out=x[:, t, :], in0=four[t % 2][:, 0:DIM], scalar=W_BACK,
                                         in1=x[:, t, :], op0=ALU.mult, op1=ALU.add).then_inc(y_free, 1)

            def norm(norm_index, taken):
                groups = TILES // 2
                for p in range(groups + 2):
                    if p < groups:
                        if taken is not None:
                            take(taken, 2 * p)
                            take(taken, 2 * p + 1)
                            dve.wait_ge(y_free, taken * TILES + (2 * (p + 1) + 2))
                        moments(norm_index, p)
                    if 1 <= p <= groups:
                        normalise(norm_index, p - 1)
                    if p >= 2:
                        split(norm_index, p - 2)

            def up(g):
                dve.tensor_scalar(bias_a[:, :], params[:, 6 * KC:6 * KC + FF_CHUNKS], W_SCALE, None, ALU.mult)\
                   .then_inc(bias_ready, 1)
                dve.wait_ge(bias_ready, g + 1)
                base = dve.snap(g * (BLKS * FF_CHUNKS))

                def low(n):
                    m, s = divmod(n, BLKS)
                    cols = slice(s * BLK, (s + 1) * BLK)
                    dve.wait_ge(inner_high, base + (n + 1))
                    dve.scalar_tensor_tensor(out=oT[1][:, m, cols], in0=inner32[:, n % 2, :], scalar=W_BACK,
                                             in1=oT[0][:, m, cols], op0=ALU.mult, op1=ALU.subtract)\
                       .then_inc(inner_low, 1)

                for n in range(BLKS * FF_CHUNKS):
                    m = n // BLKS
                    dve.wait_ge(gelu_ready, base + (n + 1))
                    if n >= 2:
                        dve.wait_ge(inner_low, base + (n - 1))
                    dve.scalar_tensor_tensor(out=inner32[:, n % 2, :], in0=four[2 * (n % 2)],
                                             scalar=bias_a[:, m:m + 1], in1=gelu32[:, n % 2, :],
                                             op0=ALU.add, op1=ALU.mult).then_inc(inner_ready, 1)
                    if n:
                        low(n - 1)
                low(BLKS * FF_CHUNKS - 1)

            with dve.Fori(0, BATCH) as b:
                dve.wait_ge(ctx_high, b + 1)
                dve.tensor_tensor(cT[1][:, 0, :], work[0][:, 0:CTX], cT[0][:, 0, :], ALU.subtract)
                dve.tensor_tensor(cT[1][0:CTX_DIM - P, 1, :], work[0][0:CTX_DIM - P, P:P + CTX],
                                  cT[0][0:CTX_DIM - P, 1, :], ALU.subtract).then_inc(ctx_split, 1)
                hold(dve, x_loaded, (b + 1) * 16)
                with dve.Fori(0, LAYERS) as l:
                    g = dve.snap(b * LAYERS + l)
                    index = dve.snap(g * 3)
                    norm(index, None)
                    end_phase(dve, g, 0)
                    attention(SELF, g)
                    end_phase(dve, g, 1)
                    dve.wait_ge(bias_added, index + (1 + CREDIT))
                    norm(dve.snap(index + 1), index)
                    end_phase(dve, g, 2)
                    attention(CROSS, g)
                    end_phase(dve, g, 3)
                    dve.wait_ge(bias_added, index + (2 + CREDIT))
                    norm(dve.snap(index + 2), dve.snap(index + 1))
                    end_phase(dve, g, 4)
                    dve.wait_ge(params_loaded, (g + 1) * 32)
                    up(g)
                    end_phase(dve, g, 5)
                    dve.wait_ge(bias_added, index + (3 + CREDIT))
                    for t in range(TILES):
                        take(dve.snap(index + 2), t)
                    end_phase(dve, g, 6)


PER_PAIR = {"self_pair": (3, 1), "cross_pair": (5, 2)}
WIDE = 2 + 4 + 2 + 2
DMAS = PAIRS * (3 + 5) + WIDE
SPLITS = PAIRS * (1 + 2) + WIDE


def kernel(**inputs):
    import concourse.bacc as bacc
    from concourse.bass_utils import run_bass_kernel_spmd

    def both(a, b):
        return np.stack([np.asarray(inputs[f"L0_xattn_{a}"]), np.asarray(inputs[f"L1_xattn_{b}"])])

    arrays = {
        "x": np.asarray(inputs["x"]), "ctx": np.asarray(inputs["ctx_768"]),
        "wq1": both("wq1", "sa_wq"), "wk1": both("wk1", "sa_wk"), "wv1": both("wv1", "sa_wv"),
        "wo1": both("wo1", "sa_wo"), "wq2": both("wq2", "ca_wq"), "wk2": both("wk2", "ca_wk"),
        "wv2": both("wv2", "ca_wv"), "wo2": both("wo2", "ca_wo"), "w1": both("w_ff1", "ff_w1"),
        "w2": both("w_ff2", "ff_w2"),
        "rows": np.stack([both("bo1", "sa_bo"), both("bo2", "ca_bo"), both("b_ff2", "ff_b2")], axis=1),
    }
    columns = [both(a, b).reshape(LAYERS, -1, P).transpose(0, 2, 1) for a, b in (
        ("g1", "ln1_g"), ("b1", "ln1_b"), ("g2", "ln2_g"), ("b2", "ln2_b"), ("g3", "ln3_g"),
        ("b3", "ln3_b"), ("b_ff1", "ff_b1"))]
    arrays["params"] = np.concatenate(columns, axis=2)

    nc = bacc.Bacc("TRN2", target_bir_lowering=False, num_devices=1)
    io, feed = {}, {}
    for name, a in arrays.items():
        feed[f"in_{name}"] = np.ascontiguousarray(a)
        io[name] = nc.dram_tensor(f"in_{name}", a.shape, mybir.dt.from_np(a.dtype), kind="ExternalInput").ap()
    io["out"] = nc.dram_tensor("out_x", (BATCH, TOKENS, DIM), F32, kind="ExternalOutput").ap()
    build(nc, io)
    result = run_bass_kernel_spmd(nc, [feed], core_ids=[0])
    return result.results[0]["out_x"]
```

```python
import collections
from contextlib import ExitStack

import numpy as np

import concourse.bass as bass
from concourse import mybir
from concourse.alu_op_type import AluOpType as ALU

F32 = mybir.dt.float32
F16 = mybir.dt.float16
ACT = mybir.ActivationFunctionType
AX = mybir.AxisListType

P = 128
BATCH, TOKENS, DIM = 2, 1024, 256
LAYERS = 2
HEADS, DH = 16, 64
INNER = HEADS * DH
CTX, CTX_DIM = 77, 192
FF = 4 * DIM
EPS = 1e-5

PAIRS = HEADS // 2
TILES = TOKENS // P
KC = DIM // P
BLK = 512
BLKS = TOKENS // BLK
W_SCALE = 64.0
W_BACK = 1.0 / W_SCALE
Q_BACK = W_BACK * DH ** -0.5
VW = 2 * DH + 1
OUT_W = DH + 1
HALF = TILES // 2
PIECE = 1024
PAIR_DMAS = 12
FF_CHUNKS = FF // P
PIECES = 10

Step = collections.namedtuple("Step", "kind step par head ahead")
WORK = ("q", "k", "v", "max", "shift", "merge")
HIGH = ("q", "k", "v", "merge")


class Shape:

    def __init__(self, name, key_tiles, key_rows, ring, polished):
        self.name, self.key_tiles, self.key_rows, self.ring = name, key_tiles, key_rows, ring
        self.own = key_tiles > 1
        self.keys = key_tiles * key_rows
        self.k_blocks = BLKS if self.own else 1
        self.v_blocks = 2 if self.own else 1
        self.polished = polished
        self.pairs_before = 0 if self.own else PAIRS
        self.fetches_before = 0 if self.own else FETCHES["self"] // 2

    def queries(self, par, ahead):
        return [Step("q", b, par, 0, ahead) for b in range(BLKS)]

    def key_blocks(self, par, ahead):
        return [Step("k", b, par, 0, ahead) for b in range(self.k_blocks)]

    def values(self, par, ahead):
        return [Step("v", b, par, 0, ahead) for b in range(self.v_blocks)]

    def maxima(self, par, head):
        first = [Step("arrive", 0, par, 0, 0)] if head == 0 else []
        if self.own:
            tiles = [[Step("max", (t, h), par, head, 0) for h in range(BLKS)] for t in range(TILES)]
        else:
            tiles = [[Step("max", (h, 0), par, head, 0) for h in range(2)]]
        tiles[0] = first + tiles[0]
        tiles[-1] = tiles[-1] + [Step("combine", 0, par, head, 0)]
        return tiles

    def low(self, s, par, head):
        return [Step("polish" if s in self.polished else "refine", s, par, head, 0)]

    def self_unit(self, par, head, before, after, project, merge, loads):
        kt = self.key_tiles
        nxt = (par, 1) if head == 0 else (1 - par, 0)
        prv = (par, 0) if head == 1 else (1 - par, 1)
        maxima = self.maxima(*nxt) if after else []
        placed = collections.defaultdict(list)
        if project and head == 0:
            placed[0] = [Step("start", 0, 1 - par, 0, 1)]
            for i, step in enumerate(self.queries(1 - par, 1) + self.key_blocks(1 - par, 1)):
                placed[1 + i].append(step)
        elif project:
            for i, step in enumerate(self.values(1 - par, 1)):
                placed[4 + i].append(step)
        if merge:
            for h in range(2):
                placed[2 + h].append(Step("merge", h, 1 - par, 0, -1))
        out = [Step("unit", 0, par, head, 0)]
        for s in range(kt):
            tiles = sum([maxima.pop(0) for _ in range(MAX_TILES[s]) if maxima], [])
            out += tiles[:-len(tiles) // 2 or None] if s else []
            out += placed[s]
            out.append(Step("score", s, par, head, 0))
            out += tiles[-len(tiles) // 2:] if s and tiles else tiles
            if s % 2 == 0 and s // 2 < len(loads):
                out.append(loads[s // 2][0])
            if s % 2 == 0 and 0 < s and s // 2 - 1 < len(loads):
                out.append(loads[s // 2 - 1][1])
            if s >= 1:
                out += self.low(s - 1, par, head)
            elif before:
                out += self.low(kt - 1, *prv)
            if s == kt - 1 and after:
                out.append(Step("shift", 0, *nxt, 0))
            if s >= 2:
                out.append(Step("value", s - 2, par, head, 0))
            elif before:
                out.append(Step("value", kt - 2 + s, *prv, 0))
                if s == 1:
                    out.append(Step("gather", 0, *prv, 0))
        return out

    def self_pair(self, par, loads, first=False, last=False):
        return (self.self_unit(par, 0, not first, True, not last, False, loads[0])
                + self.self_unit(par, 1, True, not last, not last, not first, loads[1]))

    def cross_pair(self, par, loads, first=False, maxima=True, project=True):
        other = 1 - par
        out = []
        for head in range(2):
            out += [Step("unit", 0, par, head, 0), Step("score", 0, par, head, 0)]
            if maxima:
                out += self.maxima(other, head)[0]
            if project and head == 0:
                out += [Step("start", 0, par, 0, 2), self.queries(par, 2)[0]]
            elif project:
                out += [self.queries(par, 2)[1]]
            if head == 1 or not first:
                prv = (par, 0) if head == 1 else (other, 1)
                out += [Step("value", 0, *prv, 0), Step("gather", 0, *prv, 0)]
            if project and head == 1:
                out += self.key_blocks(par, 2)
            if maxima:
                out.append(Step("shift", 0, other, head, 0))
            if maxima and head == 0:
                out += self.values(other, 1)
            out += self.low(0, par, head)
            if not first:
                out.append(Step("merge", head, other, 0, -1))
            if head == 0:
                out += [fetch for fetch, _ in loads]
            else:
                out += [split for _, split in loads]
        return out

    def tail(self, par):
        kt = self.key_tiles
        out = []
        if self.own:
            out += self.low(kt - 1, par, 1)
            out += [Step("value", kt - 2, par, 1, 0)]
        out += [Step("value", kt - 1, par, 1, 0), Step("gather", 0, par, 1, 0)]
        return out + [Step("merge", h, par, 0, 0) for h in range(2)]

    def sections(self):
        count = [0]

        def load(what, par=0, ahead=0):
            buffer = ("even", "odd")[count[0] % 2]
            count[0] += 1
            return [Step(f"{buffer} {kind}", what, par, 0, ahead) for kind in ("fetch", "split")]

        if self.own:
            head = ([Step("start", 0, 0, 0, 0)] + self.queries(0, 0) + self.key_blocks(0, 0)
                    + self.values(0, 0) + sum(self.maxima(0, 0), []) + [Step("shift", 0, 0, 0, 0)])
            last = (PAIRS - 1) % 2
            return [(head, 0, 0),
                    (self.self_pair(0, [[load(None, 0, 2), load(0)], [load(1), load(2)]], first=True), 0, 0),
                    (self.self_pair(1, [[load(None, 1, 2)], []])
                     + self.self_pair(0, [[load(None, 0, 2)], []]), 1, (PAIRS - 2) // 2),
                    (self.self_pair(last, [[load(None, last, 2), load(3)], [load(4), load(5), load(6)]],
                                    last=True) + [*load(7)] + self.tail(last), PAIRS - 1, 0)]
        head = []
        for par in range(2):
            head += [Step("start", 0, par, 0, par)] + self.queries(par, par) + self.key_blocks(par, par)
        head += self.values(0, 0)
        pair2 = load(None, 0, 2)
        head.append(pair2[0])
        for h in range(2):
            head += self.maxima(0, h)[0] + [Step("shift", 0, 0, h, 0)]
        sections = [(head, 0, 0)]
        first = self.cross_pair(0, [load(None, 1, 3)], first=True)
        at = [s.kind for s in first].index("start")
        first.insert(at, pair2[1])
        sections.append((first, 0, 0))
        sections.append((self.cross_pair(1, [load(None, 0, 3)]) + self.cross_pair(0, [load(None, 1, 3)]),
                         1, (PAIRS - 4) // 2))
        sections.append((self.cross_pair(1, [load(None, 0, 3), load(8)])
                         + self.cross_pair(0, [load(None, 1, 3), load(9)], project=False)
                         + self.cross_pair(1, [], maxima=False, project=False) + self.tail(1),
                         PAIRS - 3, 0))
        return sections


FETCHES = {"self": PAIRS + 8, "cross": PAIRS + 2}
MAX_TILES = [2, 1, 1, 1, 1, 1, 1, 0]
SELF = Shape("self", TILES, P, 4, (1, 4, 6))
CROSS = Shape("cross", 1, CTX, 4, ())


def counted(step):
    return (step.kind, "weights") if step.kind.endswith("split") and step.step is None else (step.kind,)


class Pace:

    def __init__(self, shape, phase_round):
        self.shape = shape
        self.sections = shape.sections()
        self.round = phase_round
        self.all = collections.Counter()
        for steps, _, turns in self.sections:
            for s in steps:
                for k in counted(s):
                    self.all[k] += max(turns, 1)
        self.passed = collections.Counter()
        self.turn = collections.Counter()
        self.base = {}
        self.r = None

    def walk(self, engine, do):
        for steps, pair, turns in self.sections:
            self.turn = collections.Counter(k for s in steps for k in counted(s))
            if turns:
                with engine.Fori(0, turns) as r:
                    self.r, self.base = r, {}
                    self._steps(engine, steps, do, pair, r)
                for k in self.turn:
                    self.passed[k] += self.turn[k] * (turns - 1)
            else:
                self.r, self.base = None, {}
                self._steps(engine, steps, do, pair, None)
        self.r, self.base = None, {}

    def _steps(self, engine, steps, do, pair, r):
        self.engine = engine
        at, units = pair, 0
        for s in steps:
            if s.kind == "unit":
                self.unit = s.par, s.head
                at, units = pair + units // 2, units + 1
            where = at + s.ahead
            do(s, where if r is None else r * 2 + where)
            for k in counted(s):
                self.passed[k] += 1

    def here(self, *kinds):
        return sum(self.passed[k] for k in kinds)

    def n(self, *kinds, times=1):
        key = kinds, times
        if key not in self.base:
            each, first = sum(self.all[k] for k in kinds), 0
            if kinds[0] in ("start", "weights"):
                each, first = 2 * PAIRS, self.shape.pairs_before + (2 if kinds[0] == "weights" else 0)
            elif kinds[0].split()[0] in ("even", "odd"):
                each, first = sum(FETCHES.values()) // 2, self.shape.fetches_before + 1
            base = self.round * (each * times) + first * times
            if self.r is not None:
                base = base + self.r * (sum(self.turn[k] for k in kinds) * times)
            self.base[key] = self.engine.snap(base)
        return self.base[key] + self.here(*kinds) * times

    def pairs(self, times=1):
        return self.n("arrive", times=times) + (self.here("start") - self.here("arrive")) * times

    def back(self, step):
        return 1 if (step.par, step.head) == self.unit else 2

    def tiles(self, step):
        kt = self.shape.key_tiles
        return self.n("unit", times=kt) + (step.step + 1 - self.back(step) * kt)

    def lows(self, step):
        mine = [k for k in range(self.shape.key_tiles)
                if (k in self.shape.polished) == (step.step in self.shape.polished)]
        return self.n("unit", times=len(mine)) + (sum(k <= step.step for k in mine)
                                                  - self.back(step) * len(mine))


def build(nc, io):
    ctx = ExitStack()
    with ctx:
        def sb(name, shape, dtype=F32):
            return ctx.enter_context(nc.sbuf_tensor(name, shape, dtype))

        def ps(name, columns):
            return ctx.enter_context(nc.psum_tensor(name, [P, columns], F32))

        def sem(name):
            return ctx.enter_context(nc.semaphore(name))

        scores = [ps(f"scores{i}", 2 * BLK) for i in range(2)]
        outs = [ps(f"outs{i}", BLK) for i in range(2)]
        work = [ps(f"work{i}", BLK) for i in range(2)]
        four = [scores[i][:, h * BLK:(h + 1) * BLK] for i in range(2) for h in range(2)]

        ident = sb("ident", [P, P])
        ident16 = sb("ident16", [P, P], F16)
        x = sb("x_sb", [P, TILES, DIM])
        xn = sb("xn", [P, 4, DIM])
        stats = sb("stats", [P, TILES, 6])
        mean_var = sb("mean_var", [P, TILES, 2])
        var_eps = sb("var_eps", [P, TILES])
        rstd = sb("rstd", [P, TILES])
        eps = sb("eps", [P, 2])
        minus_half = sb("minus_half", [P, 2])
        t32 = sb("t32", [P, 2, KC, 2 * P])
        hT = [sb(f"hT{i}", [P, KC, TOKENS], F16) for i in range(2)]
        cT = [sb(f"cT{i}", [P, 2, CTX], F16) for i in range(2)]
        ctx_sb = sb("ctx_sb", [CTX, CTX_DIM])
        n_par = 6 * KC + 2 * FF_CHUNKS
        params = sb("params", [P, n_par])
        bias_a = sb("bias_a", [P, FF_CHUNKS])
        rows = sb("rows", [P, 3, DIM])
        raw = {e: sb(f"raw_{e}", [P, PIECE]) for e in ("even", "odd")}
        wp = [sb(f"wp{i}", [P, 2, 6, P], F16) for i in range(2)]
        wo = [sb(f"wo{i}", [P, PAIRS, DIM], F16) for i in range(2)]
        w1 = [sb(f"w1{i}", [P, KC, 2 * FF], F16) for i in range(2)]
        w2 = [sb(f"w2{i}", [P, FF_CHUNKS, DIM], F16) for i in range(2)]
        staged = [[sb(f"staged_{a}{i}", [P, TOKENS], F16) for i in range(2)] for a in "qk"]
        qa = [[sb(f"qa{p}{i}", [P, TOKENS], F16) for i in range(2)] for p in range(2)]
        qb = [[sb(f"qb{p}{i}", [P, TOKENS], F16) for i in range(2)] for p in range(2)]
        ka = [[sb(f"ka{p}{i}", [P, TOKENS], F16) for i in range(2)] for p in range(2)]
        kb = [[sb(f"kb{p}{i}", [P, TOKENS], F16) for i in range(2)] for p in range(2)]
        vals = [sb(f"vals{p}", [P, TILES, 2, VW], F16) for p in range(2)]
        prob32 = sb("prob32", [P, 4, TOKENS])
        prob = [sb(f"prob{i}", [P, 4, TOKENS], F16) for i in range(2)]
        minima = sb("minima", [P, TILES, 2])
        shift16 = sb("shift16", [P, TILES], F16)
        shift_rows = sb("shift_rows", [TILES, P], F16)
        inv = sb("inv", [P, TILES])
        o_nat = sb("o_nat", [P, 2, TILES, P])
        oT = [sb(f"oT{i}", [P, PAIRS, TOKENS], F16) for i in range(2)]
        gelu32 = prob32[:, :, 0:BLK]
        inner32 = prob32[:, :, BLK:2 * BLK]

        consts_ready = sem("consts_ready")
        ones_ready = sem("ones_ready")
        x_loaded = sem("x_loaded")
        ctx_loaded = sem("ctx_loaded")
        params_loaded = sem("params_loaded")
        ctx_turned = sem("ctx_turned")
        ctx_high = sem("ctx_high")
        ctx_split = sem("ctx_split")
        phase_over = sem("phase_over")
        raw_loaded = {e: sem(f"raw_loaded_{e}") for e in raw}
        raw_used = {e: sem(f"raw_used_{e}") for e in raw}
        raw_scaled = {e: sem(f"raw_scaled_{e}") for e in raw}
        pair_split = sem("pair_split")
        piece_split = sem("piece_split")
        pair_projected = sem("pair_projected")
        y_full = sem("y_full")
        y_free = sem("y_free")
        moments_ready = sem("moments_ready")
        centred = sem("centred")
        var_ready = sem("var_ready")
        rstd_ready = sem("rstd_ready")
        norm_ready = sem("norm_ready")
        turned_full = sem("turned_full")
        turned_out = sem("turned_out")
        norm_split = sem("norm_split")
        bias_added = sem("bias_added")
        A = {}
        for s in (SELF, CROSS):
            names = ("work_full work_high work_free scores_full exp_done refined polished probs_used "
                     "outs_free inverse_ready heads_ready shift_combined row_ready")
            A[s.name] = collections.namedtuple("Sems", names)(*[sem(f"{s.name}_{n}") for n in names.split()])
        bias_ready = sem("bias_ready")
        up_full = sem("up_full")
        gelu_ready = sem("gelu_ready")
        inner_ready = sem("inner_ready")
        inner_high = sem("inner_high")
        inner_low = sem("inner_low")
        x_stored = sem("x_stored")

        PHASES = 7
        CREDIT = 1
        held = sem("held")
        block = ctx.enter_context(nc.Block())

        def hold(eng, sem_, value):
            eng.wait_ge(sem_, value)
            eng.sem_inc(held, 1)

        def end_phase(eng, g, index):
            eng.drain().then_inc(phase_over, 1)
            hold(eng, phase_over, g * (3 * PHASES) + (3 * (index + 1) + CREDIT))

        @block.sync
        def _(sp):
            def attention(shape, g, l):
                a, pace = A[shape.name], Pace(shape, g)
                tiles = 2 * shape.key_tiles
                first_pair = sp.snap(l * (2 * PAIRS) + shape.pairs_before)
                first_piece = sp.snap(l * PIECES)

                def spread(which, dests, step):
                    hold(sp, a.work_free, pace.n(*WORK) + 3)
                    if step.ahead:
                        sp.wait_ge(a.scores_full, pace.pairs(tiles) + (CREDIT - 2 * tiles))
                    n = TOKENS if which == 0 else shape.keys
                    for head in range(2):
                        for dest, row, part in dests:
                            sp.dma_start(dest[step.par][head][row:row + DH, 0:n],
                                         staged[which][part][head * DH:(head + 1) * DH, 0:n])\
                              .then_inc(a.heads_ready, 16)

                def do(step, pair):
                    if step.kind.endswith("fetch"):
                        e = step.kind.split()[0]
                        if step.step is None:
                            dest, source = raw[e][:, 0:6 * P], io["pairs"][bass.ds(first_pair + pair, 1), :, :]
                        else:
                            dest, source = raw[e][:, :], io["pieces"][bass.ds(first_piece + step.step, 1), :, :]
                        sp.wait_ge(raw_used[e], pace.n(step.kind))
                        sp.dma_start(dest, source.rearrange("o p n -> (o p) n")).then_inc(raw_loaded[e], 16)
                    elif step.kind == "q" and step.step == BLKS - 1:
                        spread(0, [(qa, 0, 0), (qa, DH, 0), (qb, 0, 1)], step)
                    elif step.kind == "k" and step.step == shape.k_blocks - 1:
                        spread(1, [(ka, 0, 0), (ka, DH, 1), (kb, 0, 0)], step)
                    elif step.kind == "shift":
                        sp.wait_ge(a.work_free, pace.n(*WORK) + 3)
                        sp.dma_start(qb[step.par][step.head][DH:DH + 1, :]
                                     .rearrange("o (t c) -> o t c", t=TILES),
                                     shift_rows[:, :]).then_inc(a.row_ready, 16)

                pace.walk(sp, do)

            sp.sem_inc(x_stored, CREDIT)
            for a in A.values():
                sp.sem_inc(a.heads_ready, CREDIT)
                sp.sem_inc(a.row_ready, CREDIT)
            for n, e in enumerate(raw):
                sp.dma_start(raw[e][:, 0:6 * P], io["pairs"][n, :, :]).then_inc(raw_loaded[e], 16)
            with sp.Fori(0, BATCH) as b:
                sp.wait_ge(x_stored, b * 16 + CREDIT)
                sp.dma_start(x[:, :, :], io["x"][bass.ds(b, 1), :, :]
                             .rearrange("o (t p) d -> p (o t) d", p=P)).then_inc(x_loaded, 16)
                sp.dma_start(ctx_sb[:, :], io["ctx"][bass.ds(b, 1), :, :]
                             .rearrange("o t d -> (o t) d")).then_inc(ctx_loaded, 16)
                with sp.Fori(0, LAYERS) as l:
                    g = sp.snap(b * LAYERS + l)
                    hold(sp, phase_over, g * (3 * PHASES) + CREDIT)
                    hold(sp, bias_added, g * 3 + CREDIT)
                    sp.dma_start(params[:, :], io["params"][bass.ds(l, 1), :, :]
                                 .rearrange("o p n -> (o p) n")).then_inc(params_loaded, 16)
                    sp.dma_start(rows[:, :, :], io["rows"][bass.ds(l, 1), :, :]
                                 .to_broadcast([P, 3, DIM])).then_inc(params_loaded, 16)
                    attention(SELF, g, l)
                    attention(CROSS, g, l)
                sp.wait_ge(phase_over, (b + 1) * (3 * PHASES * LAYERS) + CREDIT)
                sp.dma_start(io["out"][bass.ds(b, 1), :, :].rearrange("o (t p) d -> p (o t) d", p=P),
                             x[:, :, :]).then_inc(x_stored, 16)
            sp.wait_ge(x_stored, BATCH * 16 + CREDIT)

        @block.gpsimd
        def _(pool):
            pool.memset(ident[:, :], 0.0).then_inc(consts_ready, 1)
            pool.memset(eps[:, :], EPS).then_inc(consts_ready, 1)
            pool.memset(minus_half[:, :], -0.5).then_inc(consts_ready, 1)
            pool.wait_ge(consts_ready, 3)
            pool.affine_select(out=ident[:, :], in_=ident[:, :], compare_op=ALU.not_equal, fill=1.0,
                               base=0, pattern=[[-1, P]], channel_multiplier=1).then_inc(consts_ready, 1)
            pool.wait_ge(consts_ready, 4)
            pool.tensor_copy(ident16[:, :], ident[:, :]).then_inc(consts_ready, 1)

            def split(e, before, source, high, low, done):
                pool.tensor_scalar(high, source, W_SCALE, 1.0, ALU.mult, ALU.mult)
                pool.tensor_scalar(source, source, W_SCALE, 1.0, ALU.mult, ALU.mult)\
                    .then_inc(raw_scaled[e], 1)
                pool.wait_ge(raw_scaled[e], before + 1)
                pool.tensor_tensor(low, source, high, ALU.subtract).then_inc(raw_used[e], 1)
                pool.drain().then_inc(done, 1)

            def norm(index):
                for p in range(TILES // 2):
                    two = slice(2 * p, 2 * p + 2)
                    pool.wait_ge(moments_ready, index * TILES + 2 * (p + 1))
                    pool.tensor_tensor(var_eps[:, two], mean_var[:, two, 1], eps[:, :], ALU.add)\
                        .then_inc(var_ready, 1)
                    pool.wait_ge(var_ready, index * (TILES // 2) + (p + 1))
                    pool.tensor_tensor(rstd[:, two], var_eps[:, two], minus_half[:, :], ALU.pow)\
                        .then_inc(rstd_ready, 1)

            def add_bias(index, row):
                pool.wait_ge(norm_ready, index * TILES + TILES)
                pool.tensor_tensor(x[:, :, :], x[:, :, :],
                                   rows[:, row, :].unsqueeze(1).to_broadcast([P, TILES, DIM]), ALU.add)\
                    .then_inc(bias_added, 1)

            def split_pair(e, before, par):
                high, low = [wp[par][:, part, :, :].rearrange("p s n -> p (s n)") for part in range(2)]
                split(e, before, raw[e][:, 0:6 * P], high, low, pair_split)

            def split_piece(e, before, n):
                first, dest = next((f, d) for f, d in ((8, wo), (6, w2), (2, w1), (0, wo)) if n >= f)
                if dest is w1:
                    c, half = divmod(n - first, 2)
                    high, low = [d[:, c, half * PIECE:(half + 1) * PIECE] for d in dest]
                else:
                    rows_ = PIECE // DIM
                    high, low = [d[:, (n - first) * rows_:(n - first + 1) * rows_, :]
                                 .rearrange("p c n -> p (c n)") for d in dest]
                split(e, before, raw[e][:, :], high, low, piece_split)

            def attention(shape, g):
                a, pace = A[shape.name], Pace(shape, g)

                def do(step, pair):
                    if step.kind.endswith("split"):
                        e, n = step.kind.split()[0], step.step
                        before = pace.n(step.kind)
                        if n is None:
                            hold(pool, pair_projected, pace.n("weights") + 1)
                        elif n in (0, 8):
                            hold(pool, phase_over, g * (3 * PHASES) + (3 * (1 if n == 0 else 3) + CREDIT))
                        hold(pool, raw_loaded[e], (before + 1) * 16)
                        if n is None:
                            split_pair(e, before, step.par)
                        else:
                            split_piece(e, before, n)
                    elif step.kind == "polish":
                        slot = step.step % shape.ring
                        pool.wait_ge(a.exp_done, pace.tiles(step) + 2)
                        pool.tensor_tensor(prob[1][:, slot, :], prob32[:, slot, :], prob[0][:, slot, :],
                                           ALU.subtract).then_inc(a.polished, 1)

                pace.walk(pool, do)

            for n, e in enumerate(raw):
                hold(pool, raw_loaded[e], 16)
                split_pair(e, 0, n)
            pool.sem_inc(bias_added, CREDIT)
            with pool.Fori(0, BATCH) as b:
                with pool.Fori(0, LAYERS) as l:
                    g = pool.snap(b * LAYERS + l)
                    norm(pool.snap(g * 3))
                    pool.wait_ge(params_loaded, (g + 1) * 32)
                    add_bias(pool.snap(g * 3), 0)
                    attention(SELF, g)
                    norm(pool.snap(g * 3 + 1))
                    add_bias(pool.snap(g * 3 + 1), 1)
                    attention(CROSS, g)
                    norm(pool.snap(g * 3 + 2))
                    add_bias(pool.snap(g * 3 + 2), 2)

        @block.tensor
        def _(pe):
            pe.sem_inc(pair_projected, 2)
            for a in A.values():
                pe.sem_inc(a.scores_full, CREDIT)
            pe.sem_inc(A["self"].probs_used, SELF.ring)
            pe.sem_inc(A["cross"].probs_used, CROSS.ring)

            def three(out, left, right, first, last):
                pe.matmul(out, left[0], right[0], start=first, stop=False)
                pe.matmul(out, left[0], right[1], start=False, stop=False)
                return pe.matmul(out, left[1], right[0], start=False, stop=last)

            def attention(shape, g):
                a, pace = A[shape.name], Pace(shape, g)
                kr, kt = shape.key_rows, shape.key_tiles
                ctx_rows = (P, CTX_DIM - P)
                projected = []

                def bank():
                    pe.wait_ge(a.work_free, pace.n(*WORK) + 1)
                    return work[pace.here(*WORK) % 2]

                def weight(par, c, column, k=P):
                    return [wp[par][0:k, part, column + (c if column == 0 else 2 * c), :] for part in range(2)]

                def keys_in(c, cols, k=P):
                    source = hT if shape.own else cT
                    return [source[part][0:k, c, cols] for part in range(2)]

                def do(step, pair):
                    par, head, s = step.par, step.head, step.step
                    if step.kind == "start":
                        pe.wait_ge(pair_split, pace.n("start") + 1)
                    elif step.kind == "q":
                        out = bank()
                        for c in range(KC):
                            last = three(out[:, :], weight(par, c, 0),
                                         [hT[part][:, c, s * BLK:(s + 1) * BLK] for part in range(2)],
                                         c == 0, c == KC - 1)
                        last.then_inc(a.work_full, 1)
                    elif step.kind == "k":
                        out = bank()
                        n = min(BLK, shape.keys)
                        for c in range(2):
                            k = P if shape.own else ctx_rows[c]
                            last = three(out[:, 0:n], weight(par, c, 2, k),
                                         keys_in(c, slice(s * BLK, s * BLK + n), k), c == 0, c == 1)
                        last.then_inc(a.work_full, 1)
                    elif step.kind == "v":
                        out = bank()
                        for i in range(4 if shape.own else 1):
                            t = 4 * s + i
                            for c in range(2):
                                k = P if shape.own else ctx_rows[c]
                                last = three(out[0:kr, i * P:(i + 1) * P],
                                             keys_in(c, slice(t * kr, (t + 1) * kr), k),
                                             weight(par, c, 3, k), c == 0, c == 1)
                        last.then_inc(a.work_full, 1)
                        if s == shape.v_blocks - 1:
                            projected.append(step)
                    elif step.kind == "arrive":
                        pe.wait_ge(a.heads_ready, (pace.n("arrive") + 1) * (16 * PAIR_DMAS) + CREDIT)
                    elif step.kind == "max":
                        out = bank()
                        if shape.own:
                            t, h = s
                            last = pe.matmul(out[:, :], qa[par][head][:, t * P:(t + 1) * P],
                                             ka[par][head][:, h * BLK:(h + 1) * BLK], start=True, stop=True)
                        else:
                            for i in range(4):
                                t = 4 * s[0] + i
                                last = pe.matmul(out[:, i * CTX:(i + 1) * CTX],
                                                 qa[par][head][:, t * P:(t + 1) * P],
                                                 ka[par][head][:, 0:CTX], start=True, stop=True)
                        last.then_inc(a.work_full, 1)
                    elif step.kind == "shift":
                        out = bank()
                        pe.wait_ge(a.shift_combined, pace.n("shift") + 1)
                        pe.transpose(out[0:TILES, 0:P // 2].bitcast(F16), shift16[:, :], ident16[:, :])\
                          .then_inc(a.work_full, 1)
                    elif step.kind == "unit":
                        pe.wait_ge(a.row_ready, (pace.n("unit") + 1) * 16 + CREDIT)
                    elif step.kind == "score":
                        pe.wait_ge(a.exp_done, pace.n("score") + 1)
                        out = scores[pace.here("score") % 2]
                        cols = slice(s * kr, (s + 1) * kr)
                        for h in range(BLKS):
                            q = slice(h * BLK, (h + 1) * BLK)
                            last = pe.matmul(out[0:kr, q], ka[par][head][:, cols],
                                             qa[par][head][:, q], start=True, stop=False)
                            if projected:
                                last.then_inc(pair_projected, 1)
                                projected.clear()
                        for h in range(BLKS):
                            q = slice(h * BLK, (h + 1) * BLK)
                            last = pe.matmul(out[0:kr, q], kb[par][head][0:DH + 1, cols],
                                             qb[par][head][0:DH + 1, q], start=False, stop=True)
                        last.then_inc(a.scores_full, 1)
                    elif step.kind == "value":
                        slot = pace.here("value") % shape.ring
                        pe.wait_ge(a.polished if s in shape.polished else a.refined, pace.lows(step))
                        if s == 0:
                            pe.wait_ge(a.outs_free, pace.n("gather") * 2 + 2)
                        for t in range(TILES):
                            out = outs[t // HALF][:, (t % HALF) * OUT_W:(t % HALF + 1) * OUT_W]
                            p_hi, p_lo = [prob[i][0:kr, slot, t * P:(t + 1) * P] for i in range(2)]
                            v = vals[par][0:kr, s, head, :]
                            pe.matmul(out, p_hi, v[:, DH:VW], start=(s == 0 and t % HALF == 0),
                                      stop=False, skip_group_check=True)
                            pe.matmul(out[:, 0:DH], p_hi, v[:, 0:DH], start=False, stop=False,
                                      skip_group_check=True)
                            last = pe.matmul(out, p_lo, v[:, DH:VW], start=False,
                                             stop=(s == kt - 1), skip_group_check=True)
                        last.then_inc(a.probs_used, 1)
                    elif step.kind == "merge":
                        out = bank()
                        pe.wait_ge(a.outs_free, pace.n("merge") * 2 + (6 if s == 0 else 4))
                        for i in range(HALF):
                            last = pe.transpose(out[:, i * P:(i + 1) * P], o_nat[:, par, s * HALF + i, :],
                                                ident[:, :])
                        last.then_inc(a.work_full, 1)

                pace.walk(pe, do)

            def project(index, t, w):
                out = four[t % 2][:, 0:DIM]
                pe.wait_ge(y_free, index * TILES + (t + 1))
                for c in range(PAIRS):
                    last = three(out, [oT[part][:, c, t * P:(t + 1) * P] for part in range(2)],
                                 [w[part][:, c, :] for part in range(2)], c == 0, c == PAIRS - 1)
                last.then_inc(y_full, 1)

            def turn(index, p):
                pe.wait_ge(norm_ready, index * TILES + 2 * (p + 1))
                if p >= 2:
                    pe.wait_ge(turned_out, index * (TILES // 2) + (p - 1))
                for c in range(KC):
                    for i in range(2):
                        last = pe.transpose(work[p % 2][:, (2 * c + i) * P:(2 * c + i + 1) * P],
                                            xn[:, (2 * p + i) % 4, c * P:(c + 1) * P], ident[:, :])
                last.then_inc(turned_full, 1)

            def project_and_turn(g, k, w, pieces, norm_index):
                index = pe.snap(g * 3 + k)
                pe.wait_ge(piece_split, g * PIECES + pieces)
                for p in range(TILES // 2):
                    project(index, 2 * p, w)
                    project(index, 2 * p + 1, w)
                    if norm_index is not None and p >= 2:
                        turn(norm_index, p - 2)
                if norm_index is not None:
                    turn(norm_index, TILES // 2 - 2)
                    turn(norm_index, TILES // 2 - 1)

            def up(g):
                pe.wait_ge(piece_split, g * PIECES + 6)
                base = pe.snap(g * (BLKS * FF_CHUNKS))
                for n in range(BLKS * FF_CHUNKS):
                    m, s = divmod(n, BLKS)
                    pe.wait_ge(inner_ready, base + (n + 1))
                    for half in (1, 0):
                        out = four[2 * (n % 2) + half]
                        col = slice(half * FF + m * P, half * FF + (m + 1) * P)
                        for c in range(KC):
                            last = three(out, [w1[part][:, c, col] for part in range(2)],
                                         [hT[part][:, c, s * BLK:(s + 1) * BLK] for part in range(2)],
                                         c == 0, c == KC - 1)
                    last.then_inc(up_full, 1)

            pe.wait_ge(consts_ready, 5)
            pe.wait_ge(ones_ready, 1)
            with pe.Fori(0, BATCH) as b:
                pe.wait_ge(ctx_loaded, (b + 1) * 16)
                pe.transpose(work[0][:, 0:CTX], ctx_sb[:, 0:P], ident[0:CTX, 0:CTX])
                pe.transpose(work[0][0:CTX_DIM - P, P:P + CTX], ctx_sb[:, P:CTX_DIM],
                             ident[0:CTX, 0:CTX]).then_inc(ctx_turned, 1)
                hold(pe, ctx_split, b + 1)
                with pe.Fori(0, LAYERS) as l:
                    g = pe.snap(b * LAYERS + l)
                    for p in range(TILES // 2):
                        turn(pe.snap(g * 3), p)
                    end_phase(pe, g, 0)
                    attention(SELF, g)
                    end_phase(pe, g, 1)
                    project_and_turn(g, 0, wo, 2, pe.snap(g * 3 + 1))
                    end_phase(pe, g, 2)
                    attention(CROSS, g)
                    end_phase(pe, g, 3)
                    project_and_turn(g, 1, wo, 10, pe.snap(g * 3 + 2))
                    end_phase(pe, g, 4)
                    up(g)
                    end_phase(pe, g, 5)
                    project_and_turn(g, 2, w2, 8, None)
                    end_phase(pe, g, 6)

        @block.scalar
        def _(act):
            act.sem_inc(A["self"].exp_done, 2)
            act.sem_inc(A["cross"].exp_done, 2)

            def attention(shape, g):
                a, pace = A[shape.name], Pace(shape, g)
                kr, kt = shape.key_rows, shape.key_tiles

                def bank():
                    act.wait_ge(a.work_full, pace.n(*WORK) + 1)
                    return work[pace.here(*WORK) % 2]

                def do(step, pair):
                    par, head, s = step.par, step.head, step.step
                    if step.kind == "start":
                        act.wait_ge(a.heads_ready, pace.pairs(16 * PAIR_DMAS) + CREDIT)
                    elif step.kind in "qk":
                        out = bank()
                        n = BLK if step.kind == "q" else min(BLK, shape.keys)
                        act.activation(staged["qk".index(step.kind)][0][:, s * BLK:s * BLK + n], out[:, 0:n],
                                       ACT.Copy, scale=Q_BACK if step.kind == "q" else W_BACK)\
                           .then_inc(a.work_high, 1)
                    elif step.kind == "v":
                        out = bank()
                        tiles = 4 if shape.own else 1
                        if s == 0 and pace.here("v") >= 2 * shape.v_blocks:
                            act.wait_ge(a.probs_used, pace.n("v", times=2 * kt // shape.v_blocks)
                                        + (shape.ring - 2 * kt))
                        act.activation(vals[par][0:kr, tiles * s:tiles * (s + 1), :, DH:2 * DH],
                                       out[0:kr, 0:tiles * P].rearrange("p (t h d) -> p t h d", h=2, d=DH),
                                       ACT.Copy, scale=W_BACK).then_inc(a.work_high, 1)
                    elif step.kind == "merge":
                        out = bank()
                        act.activation(oT[0][:, bass.ds(pair, 1), s * BLK:(s + 1) * BLK]
                                       .rearrange("p o n -> p (o n)"), out[:, :], ACT.Copy)\
                           .then_inc(a.work_high, 1)
                    elif step.kind == "score":
                        n = pace.here("score")
                        source = scores[n % 2][0:kr, :]
                        act.wait_ge(a.scores_full, pace.n("score") + (1 + CREDIT))
                        act.wait_ge(a.probs_used, pace.n("score") + 1)
                        act.activation(prob32[0:kr, n % shape.ring, :], source, ACT.Exp)
                        act.activation(prob[0][0:kr, n % shape.ring, :], source, ACT.Exp)\
                           .then_inc(a.exp_done, 1)

                pace.walk(act, do)

            def norm(index, k):
                for p in range(TILES // 2):
                    act.wait_ge(turned_full, index * (TILES // 2) + (p + 1))
                    if p >= 2:
                        act.wait_ge(norm_split, index * (TILES // 2) + (p - 1))
                    for c in range(KC):
                        source = work[p % 2][:, 2 * c * P:2 * (c + 1) * P]
                        gain = params[:, 2 * k * KC + c:2 * k * KC + c + 1]
                        bias = params[:, (2 * k + 1) * KC + c:(2 * k + 1) * KC + c + 1]
                        act.activation(hT[0][:, c, 2 * p * P:2 * (p + 1) * P], source, ACT.Identity,
                                       bias=bias, scale=gain)
                        last = act.activation(t32[:, p % 2, c, :], source, ACT.Identity,
                                              bias=bias, scale=gain)
                    last.then_inc(turned_out, 1)

            def up(g):
                base = act.snap(g * (BLKS * FF_CHUNKS))

                def high(n):
                    m, s = divmod(n, BLKS)
                    act.wait_ge(inner_ready, base + (n + 3))
                    act.activation(oT[0][:, m, s * BLK:(s + 1) * BLK], inner32[:, n % 2, :], ACT.Copy,
                                   scale=W_BACK).then_inc(inner_high, 1)

                for n in range(BLKS * FF_CHUNKS):
                    m = n // BLKS
                    act.wait_ge(up_full, base + (n + 1))
                    act.wait_ge(inner_ready, base + (n + 1))
                    act.activation(gelu32[:, n % 2, :], four[2 * (n % 2) + 1], ACT.Gelu, scale=W_BACK,
                                   bias=params[:, 6 * KC + FF_CHUNKS + m:6 * KC + FF_CHUNKS + m + 1])\
                       .then_inc(gelu_ready, 1)
                    if n:
                        high(n - 1)
                high(BLKS * FF_CHUNKS - 1)

            with act.Fori(0, BATCH) as b:
                act.wait_ge(ctx_turned, b + 1)
                act.activation(cT[0][:, 0, :], work[0][:, 0:CTX], ACT.Copy)
                act.activation(cT[0][0:CTX_DIM - P, 1, :], work[0][0:CTX_DIM - P, P:P + CTX], ACT.Copy)\
                   .then_inc(ctx_high, 1)
                with act.Fori(0, LAYERS) as l:
                    g = act.snap(b * LAYERS + l)
                    act.wait_ge(params_loaded, (g + 1) * 32)
                    norm(act.snap(g * 3), 0)
                    end_phase(act, g, 0)
                    attention(SELF, g)
                    end_phase(act, g, 1)
                    norm(act.snap(g * 3 + 1), 1)
                    end_phase(act, g, 2)
                    attention(CROSS, g)
                    end_phase(act, g, 3)
                    norm(act.snap(g * 3 + 2), 2)
                    end_phase(act, g, 4)
                    up(g)
                    end_phase(act, g, 5)
                    end_phase(act, g, 6)

        @block.vector
        def _(dve):
            for p in range(2):
                for i in range(2):
                    dve.memset(kb[p][i][DH:DH + 1, :], 1.0)
                dve.memset(vals[p][:, :, :, 2 * DH:VW], 1.0)
            dve.drain().then_inc(ones_ready, 1)
            dve.wait_ge(ones_ready, 1)
            dve.sem_inc(y_free, 2)
            dve.sem_inc(phase_over, CREDIT)
            dve.sem_inc(inner_ready, 2)
            for a in A.values():
                dve.sem_inc(a.work_free, 2)
                dve.sem_inc(a.outs_free, 2)

            def attention(shape, g):
                a, pace = A[shape.name], Pace(shape, g)
                kr, kt = shape.key_rows, shape.key_tiles

                def bank():
                    dve.wait_ge(a.work_full, pace.n(*WORK) + 1)
                    return work[pace.here(*WORK) % 2]

                def do(step, pair):
                    par, head, s = step.par, step.head, step.step
                    if step.kind in HIGH:
                        dve.wait_ge(a.work_high, pace.n(*HIGH) + 1)
                        out = work[pace.here(*WORK) % 2]
                    if step.kind in ("q", "k"):
                        n = BLK if step.kind == "q" else min(BLK, shape.keys)
                        parts = staged["qk".index(step.kind)]
                        cols = slice(s * BLK, s * BLK + n)
                        dve.scalar_tensor_tensor(out=parts[1][:, cols], in0=out[:, 0:n],
                                                 scalar=Q_BACK if step.kind == "q" else W_BACK,
                                                 in1=parts[0][:, cols], op0=ALU.mult, op1=ALU.subtract)\
                           .then_inc(a.work_free, 1)
                    elif step.kind == "v":
                        n = 8 if shape.own else 2
                        v = vals[par][0:kr, :, :, :].rearrange("p t h w -> p (t h) w")[:, n * s:n * (s + 1), :]
                        dve.scalar_tensor_tensor(out=v[:, :, 0:DH],
                                                 in0=out[0:kr, 0:n * DH].rearrange("p (n d) -> p n d", d=DH),
                                                 scalar=W_BACK, in1=v[:, :, DH:2 * DH],
                                                 op0=ALU.mult, op1=ALU.subtract).then_inc(a.work_free, 1)
                    elif step.kind == "merge":
                        high, low = [oT[i][:, bass.ds(pair, 1), s * BLK:(s + 1) * BLK]
                                     .rearrange("p o n -> p (o n)") for i in range(2)]
                        dve.tensor_tensor(low, out[:, :], high, ALU.subtract).then_inc(a.work_free, 1)
                    elif step.kind == "max":
                        out = bank()
                        if shape.own:
                            t, h = s
                            dve.tensor_reduce(minima[:, t, h:h + 1], out[:, :], AX.X, ALU.max, negate=True)\
                               .then_inc(a.work_free, 1)
                        else:
                            dve.tensor_reduce(shift16[:, 4 * s[0]:4 * s[0] + 4],
                                              out[:, 0:4 * CTX].rearrange("p (t k) -> p t k", t=4),
                                              AX.X, ALU.max, negate=True).then_inc(a.work_free, 1)
                    elif step.kind == "combine":
                        if shape.own:
                            dve.wait_ge(a.work_free, pace.n(*WORK) + 2)
                            dve.tensor_reduce(shift16[:, :], minima[:, :, :], AX.X, ALU.min)\
                               .then_inc(a.shift_combined, 1)
                        else:
                            dve.wait_ge(a.work_free, pace.n(*WORK) + 2)
                            dve.sem_inc(a.shift_combined, 1)
                    elif step.kind == "shift":
                        out = bank()
                        dve.wait_ge(a.row_ready, pace.n("shift") * 16 + CREDIT)
                        dve.tensor_copy(shift_rows[:, :], out[0:TILES, 0:P // 2].bitcast(F16))\
                           .then_inc(a.work_free, 1)
                    elif step.kind == "refine":
                        slot = (s if shape.own else pace.here("refine")) % shape.ring
                        dve.wait_ge(a.exp_done, pace.tiles(step) + 2)
                        dve.tensor_tensor(prob[1][0:kr, slot, :], prob32[0:kr, slot, :],
                                          prob[0][0:kr, slot, :], ALU.subtract).then_inc(a.refined, 1)
                    elif step.kind == "gather":
                        dve.wait_ge(a.probs_used, pace.n("value") + shape.ring)
                        for h in range(2):
                            view = outs[h][:, 0:HALF * OUT_W].rearrange("p (t w) -> p t w", w=OUT_W)
                            last = dve.reciprocal(inv[:, h * HALF:(h + 1) * HALF], view[:, :, DH])
                        last.then_inc(a.inverse_ready, 1)
                        dve.wait_ge(a.inverse_ready, pace.n("gather") + 1)
                        for h in range(2):
                            view = outs[h][:, 0:HALF * OUT_W].rearrange("p (t w) -> p t w", w=OUT_W)
                            dve.tensor_tensor(
                                o_nat[:, par, h * HALF:(h + 1) * HALF, head * DH:(head + 1) * DH],
                                view[:, :, 0:DH],
                                inv[:, h * HALF:(h + 1) * HALF].unsqueeze(2).to_broadcast([P, HALF, DH]),
                                ALU.mult).then_inc(a.outs_free, 1)

                pace.walk(dve, do)

            def moments(index, p):
                for t in (2 * p, 2 * p + 1):
                    dve.bn_stats(stats[:, t, :], x[:, t, :]).then_inc(centred, 1)
                hold(dve, centred, index * TILES + 2 * (p + 1))
                for t in (2 * p, 2 * p + 1):
                    dve.bn_aggr(mean_var[:, t, :], stats[:, t, :]).then_inc(moments_ready, 1)

            def normalise(index, p):
                dve.wait_ge(rstd_ready, index * (TILES // 2) + (p + 1))
                if p >= 2:
                    dve.wait_ge(turned_full, index * (TILES // 2) + (p - 1))
                for t in (2 * p, 2 * p + 1):
                    dve.tensor_scalar(xn[:, t % 4, :], x[:, t, :], mean_var[:, t, 0:1], rstd[:, t:t + 1],
                                      ALU.subtract, ALU.mult).then_inc(norm_ready, 1)

            def split(index, p):
                dve.wait_ge(turned_out, index * (TILES // 2) + (p + 1))
                cols = slice(2 * p * P, 2 * (p + 1) * P)
                dve.tensor_tensor(hT[1][:, :, cols], t32[:, p % 2, :, :], hT[0][:, :, cols], ALU.subtract)\
                   .then_inc(norm_split, 1)

            def take(index, t):
                dve.wait_ge(y_full, index * TILES + (t + 1))
                dve.scalar_tensor_tensor(out=x[:, t, :], in0=four[t % 2][:, 0:DIM], scalar=W_BACK,
                                         in1=x[:, t, :], op0=ALU.mult, op1=ALU.add).then_inc(y_free, 1)

            def norm(norm_index, taken):
                groups = TILES // 2
                for p in range(groups + 2):
                    if p < groups:
                        if taken is not None:
                            take(taken, 2 * p)
                            take(taken, 2 * p + 1)
                            dve.wait_ge(y_free, taken * TILES + (2 * (p + 1) + 2))
                        moments(norm_index, p)
                    if 1 <= p <= groups:
                        normalise(norm_index, p - 1)
                    if p >= 2:
                        split(norm_index, p - 2)

            def up(g):
                dve.tensor_scalar(bias_a[:, :], params[:, 6 * KC:6 * KC + FF_CHUNKS], W_SCALE, None, ALU.mult)\
                   .then_inc(bias_ready, 1)
                dve.wait_ge(bias_ready, g + 1)
                base = dve.snap(g * (BLKS * FF_CHUNKS))

                def low(n):
                    m, s = divmod(n, BLKS)
                    cols = slice(s * BLK, (s + 1) * BLK)
                    dve.wait_ge(inner_high, base + (n + 1))
                    dve.scalar_tensor_tensor(out=oT[1][:, m, cols], in0=inner32[:, n % 2, :], scalar=W_BACK,
                                             in1=oT[0][:, m, cols], op0=ALU.mult, op1=ALU.subtract)\
                       .then_inc(inner_low, 1)

                for n in range(BLKS * FF_CHUNKS):
                    m = n // BLKS
                    dve.wait_ge(gelu_ready, base + (n + 1))
                    if n >= 2:
                        dve.wait_ge(inner_low, base + (n - 1))
                    dve.scalar_tensor_tensor(out=inner32[:, n % 2, :], in0=four[2 * (n % 2)],
                                             scalar=bias_a[:, m:m + 1], in1=gelu32[:, n % 2, :],
                                             op0=ALU.add, op1=ALU.mult).then_inc(inner_ready, 1)
                    if n:
                        low(n - 1)
                low(BLKS * FF_CHUNKS - 1)

            with dve.Fori(0, BATCH) as b:
                dve.wait_ge(ctx_high, b + 1)
                dve.tensor_tensor(cT[1][:, 0, :], work[0][:, 0:CTX], cT[0][:, 0, :], ALU.subtract)
                dve.tensor_tensor(cT[1][0:CTX_DIM - P, 1, :], work[0][0:CTX_DIM - P, P:P + CTX],
                                  cT[0][0:CTX_DIM - P, 1, :], ALU.subtract).then_inc(ctx_split, 1)
                hold(dve, x_loaded, (b + 1) * 16)
                with dve.Fori(0, LAYERS) as l:
                    g = dve.snap(b * LAYERS + l)
                    index = dve.snap(g * 3)
                    norm(index, None)
                    end_phase(dve, g, 0)
                    attention(SELF, g)
                    end_phase(dve, g, 1)
                    dve.wait_ge(bias_added, index + (1 + CREDIT))
                    norm(dve.snap(index + 1), index)
                    end_phase(dve, g, 2)
                    attention(CROSS, g)
                    end_phase(dve, g, 3)
                    dve.wait_ge(bias_added, index + (2 + CREDIT))
                    norm(dve.snap(index + 2), dve.snap(index + 1))
                    end_phase(dve, g, 4)
                    dve.wait_ge(params_loaded, (g + 1) * 32)
                    up(g)
                    end_phase(dve, g, 5)
                    dve.wait_ge(bias_added, index + (3 + CREDIT))
                    for t in range(TILES):
                        take(dve.snap(index + 2), t)
                    end_phase(dve, g, 6)


def kernel(**inputs):
    import concourse.bacc as bacc
    from concourse.bass_utils import run_bass_kernel_spmd

    def both(a, b):
        return np.stack([np.asarray(inputs[f"L0_xattn_{a}"]), np.asarray(inputs[f"L1_xattn_{b}"])])

    arrays = {
        "x": np.asarray(inputs["x"]), "ctx": np.asarray(inputs["ctx_768"]),
        "rows": np.stack([both("bo1", "sa_bo"), both("bo2", "ca_bo"), both("b_ff2", "ff_b2")], axis=1),
    }
    columns = [both(a, b).reshape(LAYERS, -1, P).transpose(0, 2, 1) for a, b in (
        ("g1", "ln1_g"), ("b1", "ln1_b"), ("g2", "ln2_g"), ("b2", "ln2_b"), ("g3", "ln3_g"),
        ("b3", "ln3_b"), ("b_ff1", "ff_b1"))]
    arrays["params"] = np.concatenate(columns, axis=2)

    def chunks(a, b, width):
        w = both(a, b)
        full = np.zeros((LAYERS, -(-w.shape[1] // P) * P, w.shape[2]), w.dtype)
        full[:, :w.shape[1]] = w
        return full.reshape(LAYERS, -1, P, w.shape[2] // width, width).transpose(0, 3, 2, 1, 4)

    pairs = []
    for q, k, v in ((("wq1", "sa_wq"), ("wk1", "sa_wk"), ("wv1", "sa_wv")),
                    (("wq2", "ca_wq"), ("wk2", "ca_wk"), ("wv2", "ca_wv"))):
        q, k, v = [chunks(*names, P) for names in (q, k, v)]
        pairs.append(np.concatenate([q, np.stack([k, v], axis=4).reshape(*k.shape[:3], 4, P)], axis=3))
    pairs = np.concatenate(pairs, axis=1).reshape(LAYERS * 2 * PAIRS, P, 6 * P)
    arrays["pairs"] = np.concatenate([pairs, pairs[:2]])
    pieces = []
    for names in (("wo1", "sa_wo"), ("w_ff1", "ff_w1"), ("w_ff2", "ff_w2"), ("wo2", "ca_wo")):
        w = chunks(*names, both(*names).shape[2])
        pieces.append(w.reshape(LAYERS, P, -1, PIECE).transpose(0, 2, 1, 3))
    arrays["pieces"] = np.concatenate(pieces, axis=1).reshape(LAYERS * PIECES, P, PIECE)

    nc = bacc.Bacc("TRN2", target_bir_lowering=False, num_devices=1)
    io, feed = {}, {}
    for name, a in arrays.items():
        feed[f"in_{name}"] = np.ascontiguousarray(a)
        io[name] = nc.dram_tensor(f"in_{name}", a.shape, mybir.dt.from_np(a.dtype), kind="ExternalInput").ap()
    io["out"] = nc.dram_tensor("out_x", (BATCH, TOKENS, DIM), F32, kind="ExternalOutput").ap()
    build(nc, io)
    result = run_bass_kernel_spmd(nc, [feed], core_ids=[0])
    return result.results[0]["out_x"]
```

```python
import collections
from contextlib import ExitStack

import numpy as np

import concourse.bass as bass
from concourse import mybir
from concourse.alu_op_type import AluOpType as ALU

F32 = mybir.dt.float32
F16 = mybir.dt.float16
ACT = mybir.ActivationFunctionType
AX = mybir.AxisListType

P = 128
BATCH, TOKENS, DIM = 2, 1024, 256
LAYERS = 2
HEADS, DH = 16, 64
INNER = HEADS * DH
CTX, CTX_DIM = 77, 192
FF = 4 * DIM
EPS = 1e-5

PAIRS = HEADS // 2
TILES = TOKENS // P
KC = DIM // P
BLK = 512
BLKS = TOKENS // BLK
W_SCALE = 64.0
W_BACK = 1.0 / W_SCALE
Q_BACK = W_BACK * DH ** -0.5
VW = 2 * DH + 1
OUT_W = DH + 1
HALF = TILES // 2
KEY_STEPS = TILES // 2
PIECE = 1024
FF_CHUNKS = FF // P
PIECES = 10

Step = collections.namedtuple("Step", "kind step par head ahead")
PEAK = ("max", "shift")
HIGH = ("q", "k", "v", "merge")


def take(step):
    return Step("take", (step.kind, step.step), step.par, step.head, step.ahead)


def taken(steps):
    return [s for step in steps for s in (step, take(step))]


class Shape:

    def __init__(self, name, key_tiles, key_rows, score_ring, peak_ring, high_ring, polished):
        self.name, self.key_tiles, self.key_rows = name, key_tiles, key_rows
        self.score_ring, self.peak_ring, self.high_ring = score_ring, peak_ring, high_ring
        self.ring = RING
        self.own = key_tiles > 1
        self.moves = 12 if self.own else 4
        self.v_tiles = key_tiles
        self.keys = key_tiles * key_rows
        self.k_blocks = BLKS if self.own else 1
        self.v_blocks = 2 if self.own else 1
        self.polished = polished
        self.pairs_before = 0 if self.own else PAIRS
        self.fetches_before = 0 if self.own else FETCHES["self"] // 2

    def queries(self, par, ahead):
        return [Step("q", b, par, 0, ahead) for b in range(BLKS)]

    def key_blocks(self, par, ahead):
        return [Step("k", b, par, 0, ahead) for b in range(self.k_blocks)]

    def values(self, par, ahead):
        return [Step("v", b, par, 0, ahead) for b in range(self.v_blocks)]

    def maxima(self, par, head):
        first = [Step("arrive", 0, par, 0, 0)] if head == 0 else []
        if self.own:
            tiles = [[Step("max", (t, h), par, head, 0) for h in range(BLKS)] for t in range(TILES)]
        else:
            tiles = [[Step("max", (h, 0), par, head, 0) for h in range(2)]]
        tiles[0] = first + tiles[0]
        tiles[-1] = tiles[-1] + [Step("combine", 0, par, head, 0)]
        return tiles

    def low(self, s, par, head):
        return [Step("polish" if self.by_pool(s, head) else "refine", s, par, head, 0)]

    def by_pool(self, s, head):
        return s in self.polished or not self.own

    def value(self, s, par, head):
        out = [Step("value", s, par, head, 0)]
        if s % KEY_STEPS == KEY_STEPS - 1 or not self.own:
            out.append(Step("gather", s // KEY_STEPS, par, head, 0))
        return out

    def self_unit(self, par, head, before, after, project, merge, loads):
        kt = self.key_tiles
        nxt, behind = (((par, 1), (1 - par, 0)), ((1 - par, 0), (1 - par, 1)))[head]
        prv = (par, 0) if head == 1 else (1 - par, 1)
        maxima = self.maxima(*nxt)[1:] if after else [[]] * (TILES - 1)
        maxima.append(self.maxima(*behind)[0] if after > 1 else [])
        placed = collections.defaultdict(list)
        if project and head == 0:
            placed[0] = [Step("start", 0, 1 - par, 0, 1)]
            for at, step in zip((0, 1, 2, 4), self.queries(1 - par, 1) + self.key_blocks(1 - par, 1)):
                placed[at].append(step)
        elif project:
            for at, step in zip((1, 3), self.values(1 - par, 1)):
                placed[at].append(step)
        if merge:
            for at, h in ((4, 0), (6, 1)):
                placed[at].append(Step("merge", h, 1 - par, 0, -1))
        out = [Step("unit", 0, par, head, 0)]
        for s in range(kt):
            peaks = [step for step in maxima[s] if step.kind == "max"]
            if s == kt - 1 and after:
                out.append(Step("shift", 0, *nxt, 0))
            out += [step for step in maxima[s] if step.kind == "arrive"] + peaks[:1]
            out += placed[s]
            out.append(Step("score", s, par, head, 0))
            out += [take(step) for step in placed[s] if step.kind in HIGH]
            out += peaks[1:] + [step for step in maxima[s] if step.kind == "combine"]
            if s % 2 == 0 and s // 2 < len(loads):
                out.append(loads[s // 2][0])
            if s % 2 == 0 and 0 < s and s // 2 - 1 < len(loads):
                out.append(loads[s // 2 - 1][1])
            if s >= 1:
                out += self.low(s - 1, par, head)
            elif before:
                out += self.low(kt - 1, *prv)
            if s >= LAG:
                out += self.value(s - LAG, par, head)
            elif before:
                out += self.value(kt - LAG + s, *prv)
        return out

    def self_pair(self, par, loads, first=False, last=False):
        return (self.self_unit(par, 0, not first, 1 if last else 2, not last, False, loads[0])
                + self.self_unit(par, 1, True, 0 if last else 2, not last, not first, loads[1]))

    def cross_pair(self, par, loads, first=False, maxima=True, project=True):
        other = 1 - par
        merges = [] if first else [Step("merge", half, other, 0, -1) for half in range(2)]
        values = self.values(other, 1) if maxima else []
        queries = self.queries(par, 2) if project else []
        keys = self.key_blocks(par, 2) if project else []
        a, b, combine = self.maxima(par, 1)[0]
        out = [Step("unit", 0, par, 0, 0), a, Step("score", 0, par, 0, 0), b, combine]
        if not first:
            out += self.value(0, other, 1)
        out += values + [Step("shift", 0, par, 1, 0)] + self.low(0, par, 0) + merges[:1]
        out += [take(step) for step in values] + merges[1:] + [take(step) for step in merges]
        out += [fetch for fetch, _ in loads]
        arrive, a, b, combine = self.maxima(other, 0)[0]
        out += [Step("unit", 0, par, 1, 0)] + ([arrive, a] if maxima else [])
        out += [Step("score", 0, par, 1, 0)] + ([b, combine] if maxima else [])
        if project:
            out += [Step("start", 0, par, 0, 2)] + queries[:1]
        if maxima:
            out.append(Step("shift", 0, other, 0, 0))
        out += self.value(0, par, 0) + queries[1:] + [take(step) for step in queries[:1]]
        out += keys + [take(step) for step in queries[1:] + keys] + self.low(0, par, 1)
        out += [split for _, split in loads]
        return out

    def tail(self, par):
        kt = self.key_tiles
        out = []
        if self.own:
            out += self.low(kt - 1, par, 1)
        for s in range(max(kt - LAG, 0), kt):
            out += self.value(s, par, 1)
        return out + taken([Step("merge", h, par, 0, 0) for h in range(2)])

    def sections(self):
        count = [0]

        def load(what, par=0, ahead=0):
            buffer = ("even", "odd")[count[0] % 2]
            count[0] += 1
            return [Step(f"{buffer} {kind}", what, par, 0, ahead) for kind in ("fetch", "split")]

        if self.own:
            head = ([Step("start", 0, 0, 0, 0)]
                    + taken(self.queries(0, 0) + self.key_blocks(0, 0) + self.values(0, 0))
                    + sum(self.maxima(0, 0), []) + [Step("shift", 0, 0, 0, 0)] + self.maxima(0, 1)[0])
            last = (PAIRS - 1) % 2
            return [(head, 0, 0),
                    (self.self_pair(0, [[load(None, 0, 2)], [load("own")]], first=True), 0, 0),
                    (self.self_pair(1, [[load(None, 1, 2)], [load("own")]])
                     + self.self_pair(0, [[load(None, 0, 2)], [load("own")]]), 1, (PAIRS - 2) // 2),
                    (self.self_pair(last, [[load(None, last, 2), load("own")], []], last=True)
                     + self.tail(last), PAIRS - 1, 0)]
        head = []
        for par in range(2):
            head.append(Step("start", 0, par, 0, par))
            head += taken(self.queries(par, par) + self.key_blocks(par, par))
        head += taken(self.values(0, 0))
        pair2 = load(None, 0, 2)
        head.append(pair2[0])
        head += self.maxima(0, 0)[0] + [Step("shift", 0, 0, 0, 0)]
        sections = [(head, 0, 0)]
        first = self.cross_pair(0, [load(None, 1, 3)], first=True)
        at = [s.kind for s in first].index("start")
        first.insert(at, pair2[1])
        sections.append((first, 0, 0))
        sections.append((self.cross_pair(1, [load(None, 0, 3)]) + self.cross_pair(0, [load(None, 1, 3)]),
                         1, (PAIRS - 4) // 2))
        sections.append((self.cross_pair(1, [load(None, 0, 3), load(8)])
                         + self.cross_pair(0, [load(None, 1, 3), load(9)], project=False)
                         + self.cross_pair(1, [], maxima=False, project=False) + self.tail(1),
                         PAIRS - 3, 0))
        return sections


FETCHES = {"self": PAIRS + 8, "cross": PAIRS + 2}
RING, LAG = 4, 3
SELF = Shape("self", TILES, P, 2, 2, 1, (1, 3, 5, 7))
CROSS = Shape("cross", 1, CTX, 1, 2, 2, ())


def counted(step):
    return (step.kind, "weights") if step.kind.endswith("split") and step.step is None else (step.kind,)


class Pace:

    def __init__(self, shape, phase_round):
        self.shape = shape
        self.sections = shape.sections()
        self.round = phase_round
        self.all = collections.Counter()
        for steps, _, turns in self.sections:
            for s in steps:
                for k in counted(s):
                    self.all[k] += max(turns, 1)
        self.passed = collections.Counter()
        self.turn = collections.Counter()
        self.base = {}
        self.r = None

    def walk(self, engine, do):
        for steps, pair, turns in self.sections:
            self.turn = collections.Counter(k for s in steps for k in counted(s))
            if turns:
                with engine.Fori(0, turns) as r:
                    self.r, self.base = r, {}
                    self._steps(engine, steps, do, pair, r)
                for k in self.turn:
                    self.passed[k] += self.turn[k] * (turns - 1)
            else:
                self.r, self.base = None, {}
                self._steps(engine, steps, do, pair, None)
        self.r, self.base = None, {}

    def _steps(self, engine, steps, do, pair, r):
        self.engine = engine
        at, units = pair, 0
        for s in steps:
            if s.kind == "unit":
                self.unit = s.par, s.head
                at, units = pair + units // 2, units + 1
            where = at + s.ahead
            do(s, where if r is None else r * 2 + where)
            for k in counted(s):
                self.passed[k] += 1

    def here(self, *kinds):
        return sum(self.passed[k] for k in kinds)

    def n(self, *kinds, times=1):
        each, first, turn = sum(self.all[k] for k in kinds) * times, 0, sum(self.turn[k] for k in kinds) * times
        if kinds[0] in ("start", "weights"):
            each, first = 2 * PAIRS, self.shape.pairs_before + (2 if kinds[0] == "weights" else 0)
        elif kinds[0].split()[0] in ("even", "odd"):
            each, first = sum(FETCHES.values()) // 2, self.shape.fetches_before + 1
        key = each, first, turn
        if key not in self.base:
            base = self.round * each + first
            if self.r is not None:
                base = base + self.r * turn
            self.base[key] = self.engine.snap(base)
        return self.base[key] + self.here(*kinds) * times

    def pairs(self, times=1):
        return self.n("arrive", times=times) + (self.here("start") - self.here("arrive")) * times

    def back(self, step):
        return 1 if (step.par, step.head) == self.unit else 2

    def tiles(self, step):
        kt = self.shape.key_tiles
        return self.n("unit", times=kt) + (step.step + 1 - self.back(step) * kt)

    def slot(self, step):
        return (step.step if self.shape.own else self.here("score") - 1) % self.shape.ring

    def lows(self, step):
        if not self.shape.own:
            return self.n("polish")
        mine = [k for k in range(self.shape.key_tiles)
                if (k in self.shape.polished) == (step.step in self.shape.polished)]
        return self.n("unit", times=len(mine)) + (sum(k <= step.step for k in mine)
                                                  - self.back(step) * len(mine))


def build(nc, io):
    ctx = ExitStack()
    with ctx:
        def sb(name, shape, dtype=F32):
            return ctx.enter_context(nc.sbuf_tensor(name, shape, dtype))

        def ps(name, columns):
            return ctx.enter_context(nc.psum_tensor(name, [P, columns], F32))

        def sem(name):
            return ctx.enter_context(nc.semaphore(name))

        scores = [ps(f"scores{i}", 2 * BLK) for i in range(2)]
        work = [ps(f"work{i}", BLK) for i in range(4)]
        outs = {"self": work[3:], "cross": work[2:]}
        peak = {"self": [work[0], work[2]], "cross": work[:2]}
        high = {"self": [work[1]]}
        four = [scores[i][:, h * BLK:(h + 1) * BLK] for i in range(2) for h in range(2)]
        high["cross"] = four[2:4]
        first_high = four[2:4] + four[0:2] + [work[1]]

        def high_bank(shape, n):
            if shape.own and n <= len(first_high):
                return first_high[n % len(first_high)]
            return high[shape.name][n % shape.high_ring]

        ident = sb("ident", [P, P])
        ident16 = sb("ident16", [P, P], F16)
        x = sb("x_sb", [P, TILES, DIM])
        xn = sb("xn", [P, 4, DIM])
        stats = sb("stats", [P, TILES, 6])
        mean_var = sb("mean_var", [P, TILES, 2])
        var_eps = sb("var_eps", [P, TILES])
        rstd = sb("rstd", [P, TILES])
        eps = sb("eps", [P, 2])
        scale64 = sb("scale64", [P, 1])
        minus_half = sb("minus_half", [P, 2])
        t32 = sb("t32", [P, 2, KC, 2 * P])
        hT = [sb(f"hT{i}", [P, KC, TOKENS], F16) for i in range(2)]
        cT = [sb(f"cT{i}", [P, 2, CTX], F16) for i in range(2)]
        ctx_sb = sb("ctx_sb", [CTX, CTX_DIM])
        n_par = 6 * KC + 2 * FF_CHUNKS
        params = sb("params", [P, n_par])
        bias_a = sb("bias_a", [P, FF_CHUNKS])
        rows = sb("rows", [P, 3, DIM])
        raw = {e: sb(f"raw_{e}", [P, PIECE]) for e in ("even", "odd")}
        wp = [sb(f"wp{i}", [P, 2, 6, P], F16) for i in range(2)]
        wide = [sb(f"wide{i}", [P, PAIRS, PIECE], F16) for i in range(2)]
        staged = [[sb(f"staged_{a}{i}", [P, TOKENS], F16) for i in range(2)] for a in "qk"]
        qa = [[sb(f"qa{p}{i}", [P, TOKENS], F16) for i in range(2)] for p in range(2)]
        qb = [[sb(f"qb{p}{i}", [P, TOKENS], F16) for i in range(2)] for p in range(2)]
        ka = [[sb(f"ka{p}{i}", [P, TOKENS], F16) for i in range(2)] for p in range(2)]
        kb = [[sb(f"kb{p}{i}", [P, TOKENS], F16) for i in range(2)] for p in range(2)]
        vals = [sb(f"vals{p}", [P, TILES, 2, VW], F16) for p in range(2)]
        prob32 = sb("prob32", [P, 4, TOKENS])
        prob = [sb(f"prob{i}", [P, 4, TOKENS], F16) for i in range(2)]
        minima = sb("minima", [P, TILES, 2])
        shift16 = sb("shift16", [P, TILES], F16)
        shift_rows = sb("shift_rows", [TILES, P], F16)
        inv = sb("inv", [P, TILES])
        o_nat = sb("o_nat", [P, 2, TILES, P])
        oT = [sb(f"oT{i}", [P, PAIRS, TOKENS], F16) for i in range(2)]
        gelu32 = prob32[:, :, 0:BLK]
        inner32 = prob32[:, :, BLK:2 * BLK]

        consts_ready = sem("consts_ready")
        ones_ready = sem("ones_ready")
        x_loaded = sem("x_loaded")
        ctx_loaded = sem("ctx_loaded")
        params_loaded = sem("params_loaded")
        ctx_turned = sem("ctx_turned")
        ctx_high = sem("ctx_high")
        ctx_split = sem("ctx_split")
        round_over = sem("round_over")
        raw_loaded = {e: sem(f"raw_loaded_{e}") for e in raw}
        raw_used = {e: sem(f"raw_used_{e}") for e in raw}
        raw_scaled = {e: sem(f"raw_scaled_{e}") for e in raw}
        pair_split = sem("pair_split")
        piece_split = sem("piece_split")
        pair_projected = sem("pair_projected")
        y_full = sem("y_full")
        y_free = sem("y_free")
        moments_ready = sem("moments_ready")
        centred = sem("centred")
        var_ready = sem("var_ready")
        rstd_ready = sem("rstd_ready")
        norm_ready = sem("norm_ready")
        turned_full = sem("turned_full")
        turned_out = sem("turned_out")
        norm_split = sem("norm_split")
        bias_added = sem("bias_added")
        A = {}
        for s in (SELF, CROSS):
            names = ("peak_full peak_free work_full work_high work_free scores_full exp_done refined "
                     "polished probs_used outs_free inverse_ready heads_ready shift_combined row_ready")
            A[s.name] = collections.namedtuple("Sems", names)(*[sem(f"{s.name}_{n}") for n in names.split()])
        bias_ready = sem("bias_ready")
        up_full = sem("up_full")
        gelu_ready = sem("gelu_ready")
        inner_ready = sem("inner_ready")
        inner_high = sem("inner_high")
        inner_low = sem("inner_low")
        x_stored = sem("x_stored")

        CREDIT = 1
        held = sem("held")
        block = ctx.enter_context(nc.Block())

        def hold(eng, sem_, value):
            eng.wait_ge(sem_, value)
            eng.sem_inc(held, 1)

        def end_round(eng, g):
            eng.drain().then_inc(round_over, 1)
            hold(eng, round_over, g * 3 + (3 + CREDIT))

        @block.sync
        def _(sp):
            def attention(shape, g, l):
                a, pace = A[shape.name], Pace(shape, g)
                tiles = 2 * shape.key_tiles
                first_pair = sp.snap(l * (2 * PAIRS) + shape.pairs_before)
                first_piece = sp.snap(l * PIECES)

                def spread(which, step):
                    if which == "q" and not shape.own:
                        hold(sp, a.work_high, pace.n("take") + 1)
                    else:
                        hold(sp, a.work_free, pace.n("take") + 1 + shape.high_ring)
                    if step.ahead and shape.own:
                        sp.wait_ge(a.scores_full, pace.pairs(tiles) + (CREDIT - 2 * tiles))
                    n = TOKENS if which == "q" else shape.keys
                    for head in range(2):
                        mine, others = [slice(r, r + DH) for r in (head * DH, (1 - head) * DH)]
                        up, low = [part[mine, 0:n] for part in staged["qk".index(which)]]
                        qa_, qb_, ka_, kb_ = [t[step.par][head] for t in (qa, qb, ka, kb)]
                        if shape.own and which == "q":
                            moves = [(qa_[mine, 0:n], up), (qa_[others, 0:n], up), (qb_[mine, 0:n], low)]
                        elif shape.own:
                            moves = [(ka_[mine, 0:n], up), (ka_[others, 0:n], low), (kb_[mine, 0:n], up)]
                        elif which == "q":
                            moves = [(qa_[others, 0:n], qa_[mine, 0:n])]
                        else:
                            moves = [(ka_[others, 0:n], low)]
                        for dest, source in moves:
                            sp.dma_start(dest, source).then_inc(a.heads_ready, 16)

                def do(step, pair):
                    if step.kind.endswith("fetch"):
                        e = step.kind.split()[0]
                        if step.step is None:
                            dest, source = raw[e][:, 0:6 * P], io["pairs"][bass.ds(first_pair + pair, 1), :, :]
                        else:
                            number = first_piece + (pair if step.step == "own" else step.step)
                            dest, source = raw[e][:, :], io["pieces"][bass.ds(number, 1), :, :]
                        sp.wait_ge(raw_used[e], pace.n(step.kind))
                        sp.dma_start(dest, source.rearrange("o p n -> (o p) n")).then_inc(raw_loaded[e], 16)
                    elif step.kind == "take" and step.step == ("q", BLKS - 1):
                        spread("q", step)
                    elif step.kind == "take" and step.step == ("k", shape.k_blocks - 1):
                        spread("k", step)
                    elif step.kind == "shift":
                        sp.wait_ge(a.peak_free, pace.n(*PEAK) + 1 + shape.peak_ring)
                        row = DH if step.head == 0 else 0
                        sp.dma_start(qb[step.par][step.head][row:row + 1, :]
                                     .rearrange("o (t c) -> o t c", t=TILES),
                                     shift_rows[:, :]).then_inc(a.row_ready, 16)

                pace.walk(sp, do)

            sp.sem_inc(x_stored, CREDIT)
            for a in A.values():
                sp.sem_inc(a.heads_ready, CREDIT)
                sp.sem_inc(a.row_ready, CREDIT)
            for n, e in enumerate(raw):
                sp.dma_start(raw[e][:, 0:6 * P], io["pairs"][n, :, :]).then_inc(raw_loaded[e], 16)
            with sp.Fori(0, BATCH) as b:
                sp.wait_ge(x_stored, b * 16 + CREDIT)
                sp.dma_start(x[:, :, :], io["x"][bass.ds(b, 1), :, :]
                             .rearrange("o (t p) d -> p (o t) d", p=P)).then_inc(x_loaded, 16)
                sp.dma_start(ctx_sb[:, :], io["ctx"][bass.ds(b, 1), :, :]
                             .rearrange("o t d -> (o t) d")).then_inc(ctx_loaded, 16)
                with sp.Fori(0, LAYERS) as l:
                    g = sp.snap(b * LAYERS + l)
                    hold(sp, round_over, g * 3 + CREDIT)
                    hold(sp, bias_added, g * 3 + CREDIT)
                    sp.dma_start(params[:, :], io["params"][bass.ds(l, 1), :, :]
                                 .rearrange("o p n -> (o p) n")).then_inc(params_loaded, 16)
                    sp.dma_start(rows[:, :, :], io["rows"][bass.ds(l, 1), :, :]
                                 .to_broadcast([P, 3, DIM])).then_inc(params_loaded, 16)
                    attention(SELF, g, l)
                    attention(CROSS, g, l)
                sp.wait_ge(round_over, (b + 1) * (3 * LAYERS) + CREDIT)
                sp.dma_start(io["out"][bass.ds(b, 1), :, :].rearrange("o (t p) d -> p (o t) d", p=P),
                             x[:, :, :]).then_inc(x_stored, 16)
            sp.wait_ge(x_stored, BATCH * 16 + CREDIT)

        @block.gpsimd
        def _(pool):
            pool.memset(ident[:, :], 0.0).then_inc(consts_ready, 1)
            pool.memset(eps[:, :], EPS).then_inc(consts_ready, 1)
            pool.memset(minus_half[:, :], -0.5).then_inc(consts_ready, 1)
            pool.memset(scale64[:, :], W_SCALE).then_inc(consts_ready, 1)
            pool.wait_ge(consts_ready, 4)
            pool.affine_select(out=ident[:, :], in_=ident[:, :], compare_op=ALU.not_equal, fill=1.0,
                               base=0, pattern=[[-1, P]], channel_multiplier=1).then_inc(consts_ready, 1)
            pool.wait_ge(consts_ready, 5)
            pool.tensor_copy(ident16[:, :], ident[:, :]).then_inc(consts_ready, 1)

            def split(e, before, source, high, low, done, fixed=False):
                if fixed:
                    pool.tensor_scalar(high, source, W_SCALE, 1.0, ALU.mult, ALU.mult)
                else:
                    pool.tensor_tensor(high, source, scale64[:, :].to_broadcast([P, PIECE]), ALU.mult)
                pool.tensor_scalar(source, source, W_SCALE, 1.0, ALU.mult, ALU.mult)\
                    .then_inc(raw_scaled[e], 1)
                pool.wait_ge(raw_scaled[e], before + 1)
                pool.tensor_tensor(low, source, high, ALU.subtract).then_inc(raw_used[e], 1)
                pool.drain().then_inc(done, 1)

            def norm(index):
                for p in range(TILES // 2):
                    two = slice(2 * p, 2 * p + 2)
                    pool.wait_ge(moments_ready, index * TILES + 2 * (p + 1))
                    pool.tensor_tensor(var_eps[:, two], mean_var[:, two, 1], eps[:, :], ALU.add)\
                        .then_inc(var_ready, 1)
                    pool.wait_ge(var_ready, index * (TILES // 2) + (p + 1))
                    pool.tensor_tensor(rstd[:, two], var_eps[:, two], minus_half[:, :], ALU.pow)\
                        .then_inc(rstd_ready, 1)

            def add_bias(index, row):
                pool.wait_ge(norm_ready, index * TILES + TILES)
                pool.tensor_tensor(x[:, :, :], x[:, :, :],
                                   rows[:, row, :].unsqueeze(1).to_broadcast([P, TILES, DIM]), ALU.add)\
                    .then_inc(bias_added, 1)

            def split_pair(e, before, par):
                high, low = [wp[par][:, part, :, :].rearrange("p s n -> p (s n)") for part in range(2)]
                split(e, before, raw[e][:, 0:6 * P], high, low, pair_split, fixed=True)

            def split_piece(e, before, n):
                high, low = [w[:, bass.ds(n, 1), :].rearrange("p o n -> p (o n)") for w in wide]
                split(e, before, raw[e][:, :], high, low, piece_split)

            def attention(shape, g):
                a, pace = A[shape.name], Pace(shape, g)

                def do(step, pair):
                    if step.kind.endswith("split"):
                        e, n = step.kind.split()[0], step.step
                        before = pace.n(step.kind)
                        if n is None:
                            hold(pool, pair_projected, pace.n("weights") + 1)
                        elif n == 8:
                            hold(pool, y_full, g * (3 * TILES) + TILES)
                        elif isinstance(pair, int) and pair == 0:
                            hold(pool, round_over, g * 3 + CREDIT)
                        hold(pool, raw_loaded[e], before * 16 + 16)
                        if n is None:
                            split_pair(e, before, step.par)
                        else:
                            split_piece(e, before, pair if n == "own" else n - 8)
                    elif step.kind == "polish":
                        kr, slot = shape.key_rows, pace.slot(step)
                        pool.wait_ge(a.exp_done, pace.tiles(step) + shape.score_ring)
                        pool.tensor_tensor(prob[1][0:kr, slot, :], prob32[0:kr, slot, :],
                                           prob[0][0:kr, slot, :], ALU.subtract).then_inc(a.polished, 1)

                pace.walk(pool, do)

            for n, e in enumerate(raw):
                hold(pool, raw_loaded[e], 16)
                split_pair(e, 0, n)
            pool.sem_inc(bias_added, CREDIT)
            with pool.Fori(0, BATCH) as b:
                with pool.Fori(0, LAYERS) as l:
                    g = pool.snap(b * LAYERS + l)
                    norm(pool.snap(g * 3))
                    pool.wait_ge(params_loaded, (g + 1) * 32)
                    add_bias(pool.snap(g * 3), 0)
                    attention(SELF, g)
                    norm(pool.snap(g * 3 + 1))
                    add_bias(pool.snap(g * 3 + 1), 1)
                    attention(CROSS, g)
                    norm(pool.snap(g * 3 + 2))
                    add_bias(pool.snap(g * 3 + 2), 2)

        @block.tensor
        def _(pe):
            pe.sem_inc(pair_projected, 2)
            for a in A.values():
                pe.sem_inc(a.scores_full, CREDIT)
            pe.sem_inc(A["self"].probs_used, SELF.ring)
            pe.sem_inc(A["cross"].probs_used, CROSS.ring)

            def three(out, left, right, first, last):
                pe.matmul(out, left[0], right[0], start=first, stop=False)
                pe.matmul(out, left[0], right[1], start=False, stop=False)
                return pe.matmul(out, left[1], right[0], start=False, stop=last)

            def attention(shape, g):
                a, pace = A[shape.name], Pace(shape, g)
                kr = shape.key_rows
                out_banks = len(outs[shape.name])
                ctx_rows = (P, CTX_DIM - P)
                projected = []
                norms = pe.snap(g * 3 + (0 if shape.own else 1))

                def bank():
                    n, ring = pace.here(*HIGH), shape.high_ring
                    if shape.own and n <= len(first_high):
                        ring = len(first_high)
                    if n >= ring or not shape.own:
                        pe.wait_ge(a.work_free, pace.n(*HIGH) + (1 + shape.high_ring - ring))
                    return high_bank(shape, n)

                def peak_bank():
                    pe.wait_ge(a.peak_free, pace.n(*PEAK) + 1)
                    return peak[shape.name][pace.here(*PEAK) % shape.peak_ring]

                def weight(par, c, column, k=P):
                    return [wp[par][0:k, part, column + (c if column == 0 else 2 * c), :] for part in range(2)]

                def keys_in(c, cols, k=P):
                    source = hT if shape.own else cT
                    return [source[part][0:k, c, cols] for part in range(2)]

                def do(step, pair):
                    par, head, s = step.par, step.head, step.step
                    if step.kind == "start":
                        pe.wait_ge(pair_split, pace.n("start") + 1)
                    elif step.kind == "q":
                        if pace.here("start") == 1:
                            groups = norms * (TILES // 2)
                            pe.wait_ge(norm_split, groups + 2 * (s + 1))
                        out = bank()
                        for c in range(KC):
                            last = three(out[:, :], weight(par, c, 0),
                                         [hT[part][:, c, s * BLK:(s + 1) * BLK] for part in range(2)],
                                         c == 0, c == KC - 1)
                        last.then_inc(a.work_full, 1)
                    elif step.kind == "k":
                        out = bank()
                        n = min(BLK, shape.keys)
                        for c in range(2):
                            k = P if shape.own else ctx_rows[c]
                            last = three(out[:, 0:n], weight(par, c, 2, k),
                                         keys_in(c, slice(s * BLK, s * BLK + n), k), c == 0, c == 1)
                        last.then_inc(a.work_full, 1)
                    elif step.kind == "v":
                        out = bank()
                        for i in range(4 if shape.own else 1):
                            t = 4 * s + i
                            for c in range(2):
                                k = P if shape.own else ctx_rows[c]
                                last = three(out[0:kr, i * P:(i + 1) * P],
                                             keys_in(c, slice(t * kr, (t + 1) * kr), k),
                                             weight(par, c, 3, k), c == 0, c == 1)
                        last.then_inc(a.work_full, 1)
                        if s == shape.v_blocks - 1:
                            projected.append(step)
                    elif step.kind == "arrive":
                        each = 16 * shape.moves
                        pe.wait_ge(a.heads_ready, pace.n("arrive", times=each) + (each + CREDIT))
                    elif step.kind == "max":
                        out = peak_bank()
                        if shape.own:
                            t, h = s
                            last = pe.matmul(out[:, :], qa[par][head][:, t * P:(t + 1) * P],
                                             ka[par][head][:, h * BLK:(h + 1) * BLK], start=True, stop=True)
                        else:
                            for i in range(4):
                                t = 4 * s[0] + i
                                last = pe.matmul(out[:, i * CTX:(i + 1) * CTX],
                                                 qa[par][head][:, t * P:(t + 1) * P],
                                                 ka[par][head][:, 0:CTX], start=True, stop=True)
                        last.then_inc(a.peak_full, 1)
                    elif step.kind == "shift":
                        out = peak_bank()
                        pe.wait_ge(a.shift_combined, pace.n("shift") + 1)
                        pe.transpose(out[0:TILES, 0:P // 2].bitcast(F16), shift16[:, :], ident16[:, :])\
                          .then_inc(a.peak_full, 1)
                    elif step.kind == "score":
                        if shape.own and pace.here("score") == 0:
                            pe.wait_ge(a.work_free, pace.n(*HIGH) + shape.high_ring)
                        pe.wait_ge(a.exp_done, pace.n("score") + 1)
                        out = scores[pace.here("score") % shape.score_ring]
                        q = slice(s // KEY_STEPS * BLK, (s // KEY_STEPS + 1) * BLK)
                        if shape.own:
                            parts = [(slice(k * P, (k + 1) * P), q, slice(i * BLK, (i + 1) * BLK))
                                     for i in range(2) for k in (2 * (s % KEY_STEPS) + i,)]
                        else:
                            parts = [(slice(0, kr), slice(i * BLK, (i + 1) * BLK),
                                      slice(i * BLK, (i + 1) * BLK)) for i in range(2)]
                        for keys, q, at in parts:
                            last = pe.matmul(out[0:kr, at], ka[par][head][:, keys], qa[par][head][:, q],
                                             start=True, stop=False)
                            if projected:
                                last.then_inc(pair_projected, 1)
                                projected.clear()
                        if s == 0:
                            pe.wait_ge(a.row_ready, pace.n("unit", times=16) + CREDIT)
                        rows_ = slice(0, DH + 1) if head == 0 else slice(0, P)
                        for keys, q, at in parts:
                            last = pe.matmul(out[0:kr, at], kb[par][head][rows_, keys],
                                             qb[par][head][rows_, q], start=False, stop=True)
                        last.then_inc(a.scores_full, 1)
                    elif step.kind == "value":
                        slot = pace.here("value") % shape.ring
                        pe.wait_ge(a.polished if shape.by_pool(s, head) else a.refined, pace.lows(step))
                        first = s % KEY_STEPS == 0
                        if first:
                            pe.wait_ge(a.outs_free, pace.n("gather", times=out_banks) + out_banks)
                        key_tiles = [2 * (s % KEY_STEPS) + i for i in range(2)] if shape.own else [0]
                        for i, k in enumerate(key_tiles):
                            v = vals[par][0:kr, k, head, :]
                            for t in range(HALF * out_banks):
                                out = outs[shape.name][t // HALF][:, (t % HALF) * OUT_W:(t % HALF + 1) * OUT_W]
                                cols = slice(i * BLK + t * P, i * BLK + (t + 1) * P)
                                p_hi, p_lo = [prob[n][0:kr, slot, cols] for n in range(2)]
                                pe.matmul(out, p_hi, v[:, DH:VW], start=(first and i == 0 and t % HALF == 0),
                                          stop=False, skip_group_check=True)
                                pe.matmul(out[:, 0:DH], p_hi, v[:, 0:DH], start=False, stop=False,
                                          skip_group_check=True)
                                last = pe.matmul(out, p_lo, v[:, DH:VW], start=False,
                                                 stop=(k == shape.v_tiles - 1), skip_group_check=True)
                        last.then_inc(a.probs_used, 1)
                    elif step.kind == "merge":
                        out = bank()
                        pe.wait_ge(a.outs_free, pace.n("merge", times=2) + ((3 if s == 0 else 2) + out_banks))
                        for i in range(HALF):
                            last = pe.transpose(out[:, i * P:(i + 1) * P], o_nat[:, par, s * HALF + i, :],
                                                ident[:, :])
                        last.then_inc(a.work_full, 1)

                pace.walk(pe, do)

            def project(index, t, w):
                out = four[t % 2][:, 0:DIM]
                pe.wait_ge(y_free, index * TILES + (t + 1))
                for c in range(PAIRS):
                    last = three(out, [oT[part][:, c, t * P:(t + 1) * P] for part in range(2)],
                                 [wide[part][:, w + c // 4, (c % 4) * DIM:(c % 4 + 1) * DIM]
                                  for part in range(2)], c == 0, c == PAIRS - 1)
                last.then_inc(y_full, 1)

            def turn(index, p):
                pe.wait_ge(norm_ready, index * TILES + 2 * (p + 1))
                if p >= 2:
                    pe.wait_ge(turned_out, index * (TILES // 2) + (p - 1))
                for c in range(KC):
                    for i in range(2):
                        last = pe.transpose(work[p % 2][:, (2 * c + i) * P:(2 * c + i + 1) * P],
                                            xn[:, (2 * p + i) % 4, c * P:(c + 1) * P], ident[:, :])
                last.then_inc(turned_full, 1)

            def project_and_turn(g, k, w, pieces, norm_index, ready):
                index = pe.snap(g * 3 + k)
                pe.wait_ge(*ready)
                pe.wait_ge(piece_split, g * PIECES + pieces)
                for p in range(TILES // 2):
                    project(index, 2 * p, w)
                    project(index, 2 * p + 1, w)
                    if norm_index is not None and p >= 2:
                        turn(norm_index, p - 2)
                if norm_index is not None:
                    turn(norm_index, TILES // 2 - 2)
                    turn(norm_index, TILES // 2 - 1)

            def merged(shape, g):
                steps = sum(n for kind, n in Pace(shape, g).all.items() if kind in HIGH)
                return A[shape.name].work_free, (g + 1) * steps + shape.high_ring

            def up(g):
                pe.wait_ge(piece_split, g * PIECES + 6)
                base = pe.snap(g * (BLKS * FF_CHUNKS))
                for n in range(BLKS * FF_CHUNKS):
                    m, s = divmod(n, BLKS)
                    if m == 0:
                        pe.wait_ge(norm_split, g * (3 * TILES // 2) + (TILES + 2 * (s + 1)))
                        pe.wait_ge(y_free, g * (3 * TILES) + (2 * TILES + 2))
                    pe.wait_ge(inner_ready, base + (n + 1))
                    for half in (1, 0):
                        out = four[2 * (n % 2) + half]
                        for c in range(KC):
                            last = three(out, [wide[part][:, 2 + 2 * c + half, m * P:(m + 1) * P]
                                               for part in range(2)],
                                         [hT[part][:, c, s * BLK:(s + 1) * BLK] for part in range(2)],
                                         c == 0, c == KC - 1)
                    last.then_inc(up_full, 1)

            pe.wait_ge(consts_ready, 6)
            pe.wait_ge(ones_ready, 2)
            with pe.Fori(0, BATCH) as b:
                pe.wait_ge(ctx_loaded, (b + 1) * 16)
                pe.transpose(work[0][:, 0:CTX], ctx_sb[:, 0:P], ident[0:CTX, 0:CTX])
                pe.transpose(work[0][0:CTX_DIM - P, P:P + CTX], ctx_sb[:, P:CTX_DIM],
                             ident[0:CTX, 0:CTX]).then_inc(ctx_turned, 1)
                hold(pe, ctx_split, b + 1)
                with pe.Fori(0, LAYERS) as l:
                    g = pe.snap(b * LAYERS + l)
                    for p in range(TILES // 2):
                        turn(pe.snap(g * 3), p)
                    attention(SELF, g)
                    project_and_turn(g, 0, 0, 2, pe.snap(g * 3 + 1), merged(SELF, g))
                    attention(CROSS, g)
                    project_and_turn(g, 1, 0, 10, pe.snap(g * 3 + 2), merged(CROSS, g))
                    up(g)
                    project_and_turn(g, 2, 6, 8, None,
                                     (inner_low, (g + 1) * (BLKS * FF_CHUNKS)))
                    end_round(pe, g)

        @block.scalar
        def _(act):
            act.sem_inc(A["self"].exp_done, SELF.score_ring)
            act.sem_inc(A["cross"].exp_done, CROSS.score_ring)

            def attention(shape, g):
                a, pace = A[shape.name], Pace(shape, g)
                kr, kt = shape.key_rows, shape.key_tiles

                def bank():
                    act.wait_ge(a.work_full, pace.n(*HIGH) + 1)
                    return high_bank(shape, pace.here(*HIGH))

                def do(step, pair):
                    par, head, s = step.par, step.head, step.step
                    if step.kind == "start":
                        act.wait_ge(a.heads_ready, pace.pairs(16 * shape.moves) + CREDIT)
                    elif step.kind in "qk":
                        out = bank()
                        n = BLK if step.kind == "q" else min(BLK, shape.keys)
                        if not shape.own:
                            if step.kind == "q" and s == 0 and step.ahead:
                                act.wait_ge(a.scores_full, pace.pairs(2) + (CREDIT - 4))
                            dests = (qa,) if step.kind == "q" else (ka, kb)
                            for h in range(2):
                                mine = slice(h * DH, (h + 1) * DH)
                                for dest in dests:
                                    last = act.activation(dest[par][h][mine, s * BLK:s * BLK + n],
                                                          out[mine, 0:n], ACT.Copy,
                                                          scale=Q_BACK if step.kind == "q" else W_BACK)
                            if step.kind == "q":
                                last.then_inc(a.work_high, 1)
                                return
                        act.activation(staged["qk".index(step.kind)][0][:, s * BLK:s * BLK + n], out[:, 0:n],
                                       ACT.Copy, scale=Q_BACK if step.kind == "q" else W_BACK)\
                           .then_inc(a.work_high, 1)
                    elif step.kind == "v":
                        out = bank()
                        tiles = 4 if shape.own else 1
                        if s == 0 and pace.here("v") >= 2 * shape.v_blocks:
                            act.wait_ge(a.probs_used, pace.n("v", times=2 * kt // shape.v_blocks)
                                        + (shape.ring - 2 * kt))
                        act.activation(vals[par][0:kr, tiles * s:tiles * (s + 1), :, DH:2 * DH],
                                       out[0:kr, 0:tiles * P].rearrange("p (t h d) -> p t h d", h=2, d=DH),
                                       ACT.Copy, scale=W_BACK).then_inc(a.work_high, 1)
                    elif step.kind == "merge":
                        out = bank()
                        act.activation(oT[0][:, bass.ds(pair, 1), s * BLK:(s + 1) * BLK]
                                       .rearrange("p o n -> p (o n)"), out[:, :], ACT.Copy)\
                           .then_inc(a.work_high, 1)
                    elif step.kind == "score":
                        n = pace.here("score")
                        source = scores[n % shape.score_ring][0:kr, :]
                        act.wait_ge(a.scores_full, pace.n("score") + (1 + CREDIT))
                        act.wait_ge(a.probs_used, pace.n("score") + 1)
                        act.activation(prob32[0:kr, n % shape.ring, :], source, ACT.Exp)
                        act.activation(prob[0][0:kr, n % shape.ring, :], source, ACT.Exp)\
                           .then_inc(a.exp_done, 1)

                pace.walk(act, do)

            def norm(index, k):
                for p in range(TILES // 2):
                    act.wait_ge(turned_full, index * (TILES // 2) + (p + 1))
                    if p >= 2:
                        act.wait_ge(norm_split, index * (TILES // 2) + (p - 1))
                    for c in range(KC):
                        source = work[p % 2][:, 2 * c * P:2 * (c + 1) * P]
                        gain = params[:, 2 * k * KC + c:2 * k * KC + c + 1]
                        bias = params[:, (2 * k + 1) * KC + c:(2 * k + 1) * KC + c + 1]
                        act.activation(hT[0][:, c, 2 * p * P:2 * (p + 1) * P], source, ACT.Identity,
                                       bias=bias, scale=gain)
                        last = act.activation(t32[:, p % 2, c, :], source, ACT.Identity,
                                              bias=bias, scale=gain)
                    last.then_inc(turned_out, 1)

            def up(g):
                base = act.snap(g * (BLKS * FF_CHUNKS))

                def high(n):
                    m, s = divmod(n, BLKS)
                    act.wait_ge(inner_ready, base + (n + 3))
                    act.activation(oT[0][:, m, s * BLK:(s + 1) * BLK], inner32[:, n % 2, :], ACT.Copy,
                                   scale=W_BACK).then_inc(inner_high, 1)

                for n in range(BLKS * FF_CHUNKS):
                    m = n // BLKS
                    act.wait_ge(up_full, base + (n + 1))
                    act.wait_ge(inner_ready, base + (n + 1))
                    act.activation(gelu32[:, n % 2, :], four[2 * (n % 2) + 1], ACT.Gelu, scale=W_BACK,
                                   bias=params[:, 6 * KC + FF_CHUNKS + m:6 * KC + FF_CHUNKS + m + 1])\
                       .then_inc(gelu_ready, 1)
                    if n:
                        high(n - 1)
                high(BLKS * FF_CHUNKS - 1)

            with act.Fori(0, BATCH) as b:
                act.wait_ge(ctx_turned, b + 1)
                act.activation(cT[0][:, 0, :], work[0][:, 0:CTX], ACT.Copy)
                act.activation(cT[0][0:CTX_DIM - P, 1, :], work[0][0:CTX_DIM - P, P:P + CTX], ACT.Copy)\
                   .then_inc(ctx_high, 1)
                with act.Fori(0, LAYERS) as l:
                    g = act.snap(b * LAYERS + l)
                    act.wait_ge(params_loaded, (g + 1) * 32)
                    norm(act.snap(g * 3), 0)
                    attention(SELF, g)
                    norm(act.snap(g * 3 + 1), 1)
                    attention(CROSS, g)
                    norm(act.snap(g * 3 + 2), 2)
                    up(g)
                    end_round(act, g)

        @block.vector
        def _(dve):
            for p in range(2):
                dve.memset(kb[p][0][DH:DH + 1, :], 1.0)
                for t in (kb, qb):
                    dve.memset(t[p][1][0:DH, :], 0.0)
                dve.memset(vals[p][:, :, :, 2 * DH:VW], 1.0)
            dve.drain().then_inc(ones_ready, 1)
            dve.wait_ge(ones_ready, 1)
            for p in range(2):
                dve.memset(kb[p][1][0:1, :], 1.0)
            dve.drain().then_inc(ones_ready, 1)
            dve.wait_ge(ones_ready, 2)
            dve.sem_inc(y_free, 2)
            dve.sem_inc(round_over, CREDIT)
            dve.sem_inc(inner_ready, 2)
            for shape in (SELF, CROSS):
                a = A[shape.name]
                dve.sem_inc(a.peak_free, shape.peak_ring)
                dve.sem_inc(a.work_free, shape.high_ring)
                dve.sem_inc(a.outs_free, len(outs[shape.name]))

            def attention(shape, g):
                a, pace = A[shape.name], Pace(shape, g)
                kr, kt = shape.key_rows, shape.key_tiles

                def bank():
                    dve.wait_ge(a.peak_full, pace.n(*PEAK) + 1)
                    return peak[shape.name][pace.here(*PEAK) % shape.peak_ring]

                def do(step, pair):
                    par, head, s = step.par, step.head, step.step
                    kind = step.kind
                    if kind in HIGH:
                        return
                    if kind == "take":
                        dve.wait_ge(a.work_high, pace.n("take") + 1)
                        out = high_bank(shape, pace.here("take"))
                        kind, s = s
                    if kind in ("q", "k"):
                        n = BLK if kind == "q" else min(BLK, shape.keys)
                        parts = staged["qk".index(kind)]
                        cols = slice(s * BLK, s * BLK + n)
                        if kind == "q" and not shape.own:
                            for h in range(2):
                                mine = slice(h * DH, (h + 1) * DH)
                                last = dve.scalar_tensor_tensor(
                                    out=qb[par][h][mine, cols], in0=out[mine, 0:n], scalar=Q_BACK,
                                    in1=qa[par][h][mine, cols], op0=ALU.mult, op1=ALU.subtract)
                            last.then_inc(a.work_free, 1)
                            return
                        dve.scalar_tensor_tensor(out=parts[1][:, cols], in0=out[:, 0:n],
                                                 scalar=Q_BACK if kind == "q" else W_BACK,
                                                 in1=parts[0][:, cols], op0=ALU.mult, op1=ALU.subtract)\
                           .then_inc(a.work_free, 1)
                    elif kind == "v":
                        n = 8 if shape.own else 2
                        v = vals[par][0:kr, :, :, :].rearrange("p t h w -> p (t h) w")[:, n * s:n * (s + 1), :]
                        dve.scalar_tensor_tensor(out=v[:, :, 0:DH],
                                                 in0=out[0:kr, 0:n * DH].rearrange("p (n d) -> p n d", d=DH),
                                                 scalar=W_BACK, in1=v[:, :, DH:2 * DH],
                                                 op0=ALU.mult, op1=ALU.subtract).then_inc(a.work_free, 1)
                    elif kind == "merge":
                        upper, lower = [oT[i][:, bass.ds(pair, 1), s * BLK:(s + 1) * BLK]
                                     .rearrange("p o n -> p (o n)") for i in range(2)]
                        dve.tensor_tensor(lower, out[:, :], upper, ALU.subtract).then_inc(a.work_free, 1)
                    elif step.kind == "max":
                        out = bank()
                        if shape.own:
                            t, h = s
                            if s == (0, 0) and pace.here("combine"):
                                dve.wait_ge(a.shift_combined, pace.n("combine"))
                            dve.tensor_reduce(minima[:, t, h:h + 1], out[:, :], AX.X, ALU.max, negate=True)\
                               .then_inc(a.peak_free, 1)
                        else:
                            dve.tensor_reduce(shift16[:, 4 * s[0]:4 * s[0] + 4],
                                              out[:, 0:4 * CTX].rearrange("p (t k) -> p t k", t=4),
                                              AX.X, ALU.max, negate=True).then_inc(a.peak_free, 1)
                    elif step.kind == "combine":
                        if shape.own:
                            dve.wait_ge(a.peak_free, pace.n(*PEAK) + shape.peak_ring)
                            dve.tensor_reduce(shift16[:, :], minima[:, :, :], AX.X, ALU.min)\
                               .then_inc(a.shift_combined, 1)
                        else:
                            dve.wait_ge(a.peak_free, pace.n(*PEAK) + shape.peak_ring)
                            dve.sem_inc(a.shift_combined, 1)
                    elif step.kind == "shift":
                        out = bank()
                        dve.wait_ge(a.row_ready, pace.n("shift", times=16) + CREDIT)
                        dve.tensor_copy(shift_rows[:, :], out[0:TILES, 0:P // 2].bitcast(F16))\
                           .then_inc(a.peak_free, 1)
                    elif step.kind == "refine":
                        slot = pace.slot(step)
                        dve.wait_ge(a.exp_done, pace.tiles(step) + shape.score_ring)
                        dve.tensor_tensor(prob[1][0:kr, slot, :], prob32[0:kr, slot, :],
                                          prob[0][0:kr, slot, :], ALU.subtract).then_inc(a.refined, 1)
                    elif step.kind == "gather":
                        dve.wait_ge(a.probs_used, pace.n("value") + shape.ring)
                        halves = [(s, outs["self"][0])] if shape.own else list(enumerate(outs["cross"]))
                        views = [(h, bank_[:, 0:HALF * OUT_W].rearrange("p (t w) -> p t w", w=OUT_W))
                                 for h, bank_ in halves]
                        for h, view in views:
                            last = dve.reciprocal(inv[:, h * HALF:(h + 1) * HALF], view[:, :, DH])
                        last.then_inc(a.inverse_ready, 1)
                        dve.wait_ge(a.inverse_ready, pace.n("gather") + 1)
                        for h, view in views:
                            dve.tensor_tensor(
                                o_nat[:, par, h * HALF:(h + 1) * HALF, head * DH:(head + 1) * DH],
                                view[:, :, 0:DH],
                                inv[:, h * HALF:(h + 1) * HALF].unsqueeze(2).to_broadcast([P, HALF, DH]),
                                ALU.mult).then_inc(a.outs_free, 1)

                pace.walk(dve, do)

            def moments(index, p):
                for t in (2 * p, 2 * p + 1):
                    dve.bn_stats(stats[:, t, :], x[:, t, :]).then_inc(centred, 1)
                hold(dve, centred, index * TILES + 2 * (p + 1))
                for t in (2 * p, 2 * p + 1):
                    dve.bn_aggr(mean_var[:, t, :], stats[:, t, :]).then_inc(moments_ready, 1)

            def normalise(index, p):
                dve.wait_ge(rstd_ready, index * (TILES // 2) + (p + 1))
                if p >= 2:
                    dve.wait_ge(turned_full, index * (TILES // 2) + (p - 1))
                for t in (2 * p, 2 * p + 1):
                    dve.tensor_scalar(xn[:, t % 4, :], x[:, t, :], mean_var[:, t, 0:1], rstd[:, t:t + 1],
                                      ALU.subtract, ALU.mult).then_inc(norm_ready, 1)

            def split(index, p):
                dve.wait_ge(turned_out, index * (TILES // 2) + (p + 1))
                cols = slice(2 * p * P, 2 * (p + 1) * P)
                dve.tensor_tensor(hT[1][:, :, cols], t32[:, p % 2, :, :], hT[0][:, :, cols], ALU.subtract)\
                   .then_inc(norm_split, 1)

            def take(index, t):
                dve.wait_ge(y_full, index * TILES + (t + 1))
                dve.scalar_tensor_tensor(out=x[:, t, :], in0=four[t % 2][:, 0:DIM], scalar=W_BACK,
                                         in1=x[:, t, :], op0=ALU.mult, op1=ALU.add).then_inc(y_free, 1)

            def norm(norm_index, taken):
                groups = TILES // 2
                for p in range(groups + 2):
                    if p < groups:
                        if taken is not None:
                            take(taken, 2 * p)
                            take(taken, 2 * p + 1)
                            dve.wait_ge(y_free, taken * TILES + (2 * (p + 1) + 2))
                        moments(norm_index, p)
                    if 1 <= p <= groups:
                        normalise(norm_index, p - 1)
                    if p >= 2:
                        split(norm_index, p - 2)

            def up(g):
                dve.tensor_scalar(bias_a[:, :], params[:, 6 * KC:6 * KC + FF_CHUNKS], W_SCALE, None, ALU.mult)\
                   .then_inc(bias_ready, 1)
                dve.wait_ge(bias_ready, g + 1)
                base = dve.snap(g * (BLKS * FF_CHUNKS))

                def low(n):
                    m, s = divmod(n, BLKS)
                    cols = slice(s * BLK, (s + 1) * BLK)
                    dve.wait_ge(inner_high, base + (n + 1))
                    dve.scalar_tensor_tensor(out=oT[1][:, m, cols], in0=inner32[:, n % 2, :], scalar=W_BACK,
                                             in1=oT[0][:, m, cols], op0=ALU.mult, op1=ALU.subtract)\
                       .then_inc(inner_low, 1)

                for n in range(BLKS * FF_CHUNKS):
                    m = n // BLKS
                    dve.wait_ge(gelu_ready, base + (n + 1))
                    if n >= 2:
                        dve.wait_ge(inner_low, base + (n - 1))
                    dve.scalar_tensor_tensor(out=inner32[:, n % 2, :], in0=four[2 * (n % 2)],
                                             scalar=bias_a[:, m:m + 1], in1=gelu32[:, n % 2, :],
                                             op0=ALU.add, op1=ALU.mult).then_inc(inner_ready, 1)
                    if n:
                        low(n - 1)
                low(BLKS * FF_CHUNKS - 1)

            with dve.Fori(0, BATCH) as b:
                dve.wait_ge(ctx_high, b + 1)
                dve.tensor_tensor(cT[1][:, 0, :], work[0][:, 0:CTX], cT[0][:, 0, :], ALU.subtract)
                dve.tensor_tensor(cT[1][0:CTX_DIM - P, 1, :], work[0][0:CTX_DIM - P, P:P + CTX],
                                  cT[0][0:CTX_DIM - P, 1, :], ALU.subtract).then_inc(ctx_split, 1)
                hold(dve, x_loaded, (b + 1) * 16)
                with dve.Fori(0, LAYERS) as l:
                    g = dve.snap(b * LAYERS + l)
                    index = dve.snap(g * 3)
                    norm(index, None)
                    attention(SELF, g)
                    dve.wait_ge(bias_added, index + (1 + CREDIT))
                    norm(dve.snap(index + 1), index)
                    attention(CROSS, g)
                    dve.wait_ge(bias_added, index + (2 + CREDIT))
                    norm(dve.snap(index + 2), dve.snap(index + 1))
                    dve.wait_ge(params_loaded, (g + 1) * 32)
                    up(g)
                    dve.wait_ge(bias_added, index + (3 + CREDIT))
                    for t in range(TILES):
                        take(dve.snap(index + 2), t)
                    end_round(dve, g)


def kernel(**inputs):
    import concourse.bacc as bacc
    from concourse.bass_utils import run_bass_kernel_spmd

    def both(a, b):
        return np.stack([np.asarray(inputs[f"L0_xattn_{a}"]), np.asarray(inputs[f"L1_xattn_{b}"])])

    arrays = {
        "x": np.asarray(inputs["x"]), "ctx": np.asarray(inputs["ctx_768"]),
        "rows": np.stack([both("bo1", "sa_bo"), both("bo2", "ca_bo"), both("b_ff2", "ff_b2")], axis=1),
    }
    columns = [both(a, b).reshape(LAYERS, -1, P).transpose(0, 2, 1) for a, b in (
        ("g1", "ln1_g"), ("b1", "ln1_b"), ("g2", "ln2_g"), ("b2", "ln2_b"), ("g3", "ln3_g"),
        ("b3", "ln3_b"), ("b_ff1", "ff_b1"))]
    arrays["params"] = np.concatenate(columns, axis=2)

    def chunks(a, b, width):
        w = both(a, b)
        full = np.zeros((LAYERS, -(-w.shape[1] // P) * P, w.shape[2]), w.dtype)
        full[:, :w.shape[1]] = w
        return full.reshape(LAYERS, -1, P, w.shape[2] // width, width).transpose(0, 3, 2, 1, 4)

    pairs = []
    for q, k, v in ((("wq1", "sa_wq"), ("wk1", "sa_wk"), ("wv1", "sa_wv")),
                    (("wq2", "ca_wq"), ("wk2", "ca_wk"), ("wv2", "ca_wv"))):
        q, k, v = [chunks(*names, P) for names in (q, k, v)]
        pairs.append(np.concatenate([q, np.stack([k, v], axis=4).reshape(*k.shape[:3], 4, P)], axis=3))
    pairs = np.concatenate(pairs, axis=1).reshape(LAYERS * 2 * PAIRS, P, 6 * P)
    arrays["pairs"] = np.concatenate([pairs, pairs[:2]])
    pieces = []
    for names in (("wo1", "sa_wo"), ("w_ff1", "ff_w1"), ("w_ff2", "ff_w2"), ("wo2", "ca_wo")):
        w = chunks(*names, both(*names).shape[2])
        pieces.append(w.reshape(LAYERS, P, -1, PIECE).transpose(0, 2, 1, 3))
    arrays["pieces"] = np.concatenate(pieces, axis=1).reshape(LAYERS * PIECES, P, PIECE)

    nc = bacc.Bacc("TRN2", target_bir_lowering=False, num_devices=1)
    io, feed = {}, {}
    for name, a in arrays.items():
        feed[f"in_{name}"] = np.ascontiguousarray(a)
        io[name] = nc.dram_tensor(f"in_{name}", a.shape, mybir.dt.from_np(a.dtype), kind="ExternalInput").ap()
    io["out"] = nc.dram_tensor("out_x", (BATCH, TOKENS, DIM), F32, kind="ExternalOutput").ap()
    build(nc, io)
    result = run_bass_kernel_spmd(nc, [feed], core_ids=[0])
    return result.results[0]["out_x"]
```
